# Optimizing a Trainium2 kernel written in Bass

```python
import numpy as np
import jax
import jax.numpy as jnp

def _softmax(x, axis=-1):
    return jax.nn.softmax(x, axis=axis)

def _gelu(x):
    return jax.nn.gelu(x, approximate=True)

def _silu(x):
    return jax.nn.silu(x)

def _sigmoid(x):
    return jax.nn.sigmoid(x)

def _layernorm(x, axis=-1, eps=1e-05):
    m = jnp.mean(x, axis=axis, keepdims=True)
    v = jnp.var(x, axis=axis, keepdims=True)
    return (x - m) / jnp.sqrt(v + eps)

def _scatter_add(tgt, idx, src, axis=0):
    return tgt.at[idx].add(src)

def _segment_sum(src, seg, n):
    return jax.ops.segment_sum(src, seg, n)
kernel_name = 'mk_rec_standalone_d1_rec_r8_657099'

def setup_inputs(seed: int=0):
    np.random.seed(seed)
    _w = jnp.asarray

    def _rec_inputs():
        import jax
        import jax.numpy as jnp
        _rk = jax.random.key(seed)
        r_item_his = jnp.stack([jax.random.randint(jax.random.fold_in(jax.random.fold_in(_rk, 1), 0), (512,), 2649, 997334, jnp.int32), jax.random.randint(jax.random.fold_in(jax.random.fold_in(_rk, 1), 1), (512,), 3597, 999157, jnp.int32), jax.random.randint(jax.random.fold_in(jax.random.fold_in(_rk, 1), 2), (512,), 1278, 998276, jnp.int32), jax.random.randint(jax.random.fold_in(jax.random.fold_in(_rk, 1), 3), (512,), 131, 999878, jnp.int32), jax.random.randint(jax.random.fold_in(jax.random.fold_in(_rk, 1), 4), (512,), 122, 999404, jnp.int32), jax.random.randint(jax.random.fold_in(jax.random.fold_in(_rk, 1), 5), (512,), 2270, 996723, jnp.int32), jax.random.randint(jax.random.fold_in(jax.random.fold_in(_rk, 1), 6), (512,), 699, 999948, jnp.int32), jax.random.randint(jax.random.fold_in(jax.random.fold_in(_rk, 1), 7), (512,), 148, 997163, jnp.int32), jax.random.randint(jax.random.fold_in(jax.random.fold_in(_rk, 1), 8), (512,), 3, 999659, jnp.int32), jax.random.randint(jax.random.fold_in(jax.random.fold_in(_rk, 1), 9), (512,), 554, 999279, jnp.int32), jax.random.randint(jax.random.fold_in(jax.random.fold_in(_rk, 1), 10), (512,), 2327, 999381, jnp.int32), jax.random.randint(jax.random.fold_in(jax.random.fold_in(_rk, 1), 11), (512,), 897, 124994, jnp.int32), jax.random.randint(jax.random.fold_in(jax.random.fold_in(_rk, 1), 12), (512,), 1760, 999811, jnp.int32), jax.random.randint(jax.random.fold_in(jax.random.fold_in(_rk, 1), 13), (512,), 932, 998703, jnp.int32), jax.random.randint(jax.random.fold_in(jax.random.fold_in(_rk, 1), 14), (512,), 799, 124979, jnp.int32), jax.random.randint(jax.random.fold_in(jax.random.fold_in(_rk, 1), 15), (512,), 632, 999853, jnp.int32), jax.random.randint(jax.random.fold_in(jax.random.fold_in(_rk, 1), 16), (512,), 522, 997098, jnp.int32), jax.random.randint(jax.random.fold_in(jax.random.fold_in(_rk, 1), 17), (512,), 1924, 999378, jnp.int32), jax.random.randint(jax.random.fold_in(jax.random.fold_in(_rk, 1), 18), (512,), 512, 999291, jnp.int32), jax.random.randint(jax.random.fold_in(jax.random.fold_in(_rk, 1), 19), (512,), 660, 999817, jnp.int32), jax.random.randint(jax.random.fold_in(jax.random.fold_in(_rk, 1), 20), (512,), 3405, 998706, jnp.int32), jax.random.randint(jax.random.fold_in(jax.random.fold_in(_rk, 1), 21), (512,), 4945, 999883, jnp.int32), jax.random.randint(jax.random.fold_in(jax.random.fold_in(_rk, 1), 22), (512,), 395, 998190, jnp.int32), jax.random.randint(jax.random.fold_in(jax.random.fold_in(_rk, 1), 23), (512,), 925, 999788, jnp.int32), jax.random.randint(jax.random.fold_in(jax.random.fold_in(_rk, 1), 24), (512,), 433, 999210, jnp.int32), jax.random.randint(jax.random.fold_in(jax.random.fold_in(_rk, 1), 25), (512,), 2386, 996883, jnp.int32), jax.random.randint(jax.random.fold_in(jax.random.fold_in(_rk, 1), 26), (512,), 5325, 999921, jnp.int32), jax.random.randint(jax.random.fold_in(jax.random.fold_in(_rk, 1), 27), (512,), 172, 998739, jnp.int32), jax.random.randint(jax.random.fold_in(jax.random.fold_in(_rk, 1), 28), (512,), 492, 999412, jnp.int32), jax.random.randint(jax.random.fold_in(jax.random.fold_in(_rk, 1), 29), (512,), 19, 997579, jnp.int32), jax.random.randint(jax.random.fold_in(jax.random.fold_in(_rk, 1), 30), (512,), 945, 995629, jnp.int32), jax.random.randint(jax.random.fold_in(jax.random.fold_in(_rk, 1), 31), (512,), 314, 124982, jnp.int32), jax.random.randint(jax.random.fold_in(jax.random.fold_in(_rk, 1), 32), (512,), 172, 999807, jnp.int32), jax.random.randint(jax.random.fold_in(jax.random.fold_in(_rk, 1), 33), (512,), 428, 999509, jnp.int32), jax.random.randint(jax.random.fold_in(jax.random.fold_in(_rk, 1), 34), (512,), 145, 998321, jnp.int32), jax.random.randint(jax.random.fold_in(jax.random.fold_in(_rk, 1), 35), (512,), 3946, 998700, jnp.int32), jax.random.randint(jax.random.fold_in(jax.random.fold_in(_rk, 1), 36), (512,), 449, 124957, jnp.int32), jax.random.randint(jax.random.fold_in(jax.random.fold_in(_rk, 1), 37), (512,), 2079, 999379, jnp.int32), jax.random.randint(jax.random.fold_in(jax.random.fold_in(_rk, 1), 38), (512,), 427, 999385, jnp.int32), jax.random.randint(jax.random.fold_in(jax.random.fold_in(_rk, 1), 39), (512,), 1366, 998791, jnp.int32), jax.random.randint(jax.random.fold_in(jax.random.fold_in(_rk, 1), 40), (512,), 561, 124917, jnp.int32), jax.random.randint(jax.random.fold_in(jax.random.fold_in(_rk, 1), 41), (512,), 2161, 998420, jnp.int32), jax.random.randint(jax.random.fold_in(jax.random.fold_in(_rk, 1), 42), (512,), 672, 999945, jnp.int32), jax.random.randint(jax.random.fold_in(jax.random.fold_in(_rk, 1), 43), (512,), 150, 998221, jnp.int32), jax.random.randint(jax.random.fold_in(jax.random.fold_in(_rk, 1), 44), (512,), 1214, 999293, jnp.int32), jax.random.randint(jax.random.fold_in(jax.random.fold_in(_rk, 1), 45), (512,), 389, 124777, jnp.int32), jax.random.randint(jax.random.fold_in(jax.random.fold_in(_rk, 1), 46), (512,), 286, 999263, jnp.int32), jax.random.randint(jax.random.fold_in(jax.random.fold_in(_rk, 1), 47), (512,), 200, 998443, jnp.int32), jax.random.randint(jax.random.fold_in(jax.random.fold_in(_rk, 1), 48), (512,), 881, 999691, jnp.int32), jax.random.randint(jax.random.fold_in(jax.random.fold_in(_rk, 1), 49), (512,), 1406, 998212, jnp.int32), jax.random.randint(jax.random.fold_in(jax.random.fold_in(_rk, 1), 50), (512,), 677, 999794, jnp.int32), jax.random.randint(jax.random.fold_in(jax.random.fold_in(_rk, 1), 51), (512,), 2574, 999623, jnp.int32), jax.random.randint(jax.random.fold_in(jax.random.fold_in(_rk, 1), 52), (512,), 766, 124731, jnp.int32), jax.random.randint(jax.random.fold_in(jax.random.fold_in(_rk, 1), 53), (512,), 949, 999439, jnp.int32), jax.random.randint(jax.random.fold_in(jax.random.fold_in(_rk, 1), 54), (512,), 409, 999701, jnp.int32), jax.random.randint(jax.random.fold_in(jax.random.fold_in(_rk, 1), 55), (512,), 295, 999737, jnp.int32), jax.random.randint(jax.random.fold_in(jax.random.fold_in(_rk, 1), 56), (512,), 79, 999483, jnp.int32), jax.random.randint(jax.random.fold_in(jax.random.fold_in(_rk, 1), 57), (512,), 232, 998618, jnp.int32), jax.random.randint(jax.random.fold_in(jax.random.fold_in(_rk, 1), 58), (512,), 652, 999446, jnp.int32), jax.random.randint(jax.random.fold_in(jax.random.fold_in(_rk, 1), 59), (512,), 492, 997599, jnp.int32), jax.random.randint(jax.random.fold_in(jax.random.fold_in(_rk, 1), 60), (512,), 149, 999078, jnp.int32), jax.random.randint(jax.random.fold_in(jax.random.fold_in(_rk, 1), 61), (512,), 877, 124993, jnp.int32), jax.random.randint(jax.random.fold_in(jax.random.fold_in(_rk, 1), 62), (512,), 648, 999627, jnp.int32), jax.random.randint(jax.random.fold_in(jax.random.fold_in(_rk, 1), 63), (512,), 104, 999987, jnp.int32), jax.random.randint(jax.random.fold_in(jax.random.fold_in(_rk, 1), 64), (512,), 1371, 999715, jnp.int32), jax.random.randint(jax.random.fold_in(jax.random.fold_in(_rk, 1), 65), (512,), 1554, 997902, jnp.int32), jax.random.randint(jax.random.fold_in(jax.random.fold_in(_rk, 1), 66), (512,), 1429, 998779, jnp.int32), jax.random.randint(jax.random.fold_in(jax.random.fold_in(_rk, 1), 67), (512,), 6, 997549, jnp.int32), jax.random.randint(jax.random.fold_in(jax.random.fold_in(_rk, 1), 68), (512,), 11, 998566, jnp.int32), jax.random.randint(jax.random.fold_in(jax.random.fold_in(_rk, 1), 69), (512,), 224, 998830, jnp.int32), jax.random.randint(jax.random.fold_in(jax.random.fold_in(_rk, 1), 70), (512,), 1180, 998851, jnp.int32), jax.random.randint(jax.random.fold_in(jax.random.fold_in(_rk, 1), 71), (512,), 307, 997119, jnp.int32), jax.random.randint(jax.random.fold_in(jax.random.fold_in(_rk, 1), 72), (512,), 1061, 999954, jnp.int32), jax.random.randint(jax.random.fold_in(jax.random.fold_in(_rk, 1), 73), (512,), 1930, 995241, jnp.int32), jax.random.randint(jax.random.fold_in(jax.random.fold_in(_rk, 1), 74), (512,), 684, 999346, jnp.int32), jax.random.randint(jax.random.fold_in(jax.random.fold_in(_rk, 1), 75), (512,), 2923, 997923, jnp.int32), jax.random.randint(jax.random.fold_in(jax.random.fold_in(_rk, 1), 76), (512,), 3948, 124874, jnp.int32), jax.random.randint(jax.random.fold_in(jax.random.fold_in(_rk, 1), 77), (512,), 48, 999949, jnp.int32), jax.random.randint(jax.random.fold_in(jax.random.fold_in(_rk, 1), 78), (512,), 1068, 999061, jnp.int32), jax.random.randint(jax.random.fold_in(jax.random.fold_in(_rk, 1), 79), (512,), 939, 999937, jnp.int32), jax.random.randint(jax.random.fold_in(jax.random.fold_in(_rk, 1), 80), (512,), 171, 999563, jnp.int32), jax.random.randint(jax.random.fold_in(jax.random.fold_in(_rk, 1), 81), (512,), 3302, 997436, jnp.int32), jax.random.randint(jax.random.fold_in(jax.random.fold_in(_rk, 1), 82), (512,), 1251, 999713, jnp.int32), jax.random.randint(jax.random.fold_in(jax.random.fold_in(_rk, 1), 83), (512,), 2222, 999947, jnp.int32), jax.random.randint(jax.random.fold_in(jax.random.fold_in(_rk, 1), 84), (512,), 387, 999316, jnp.int32), jax.random.randint(jax.random.fold_in(jax.random.fold_in(_rk, 1), 85), (512,), 408, 997828, jnp.int32), jax.random.randint(jax.random.fold_in(jax.random.fold_in(_rk, 1), 86), (512,), 1346, 124881, jnp.int32), jax.random.randint(jax.random.fold_in(jax.random.fold_in(_rk, 1), 87), (512,), 1951, 997697, jnp.int32), jax.random.randint(jax.random.fold_in(jax.random.fold_in(_rk, 1), 88), (512,), 218, 999705, jnp.int32), jax.random.randint(jax.random.fold_in(jax.random.fold_in(_rk, 1), 89), (512,), 619, 998070, jnp.int32), jax.random.randint(jax.random.fold_in(jax.random.fold_in(_rk, 1), 90), (512,), 1542, 998531, jnp.int32), jax.random.randint(jax.random.fold_in(jax.random.fold_in(_rk, 1), 91), (512,), 695, 999785, jnp.int32), jax.random.randint(jax.random.fold_in(jax.random.fold_in(_rk, 1), 92), (512,), 6869, 997301, jnp.int32), jax.random.randint(jax.random.fold_in(jax.random.fold_in(_rk, 1), 93), (512,), 712, 999094, jnp.int32), jax.random.randint(jax.random.fold_in(jax.random.fold_in(_rk, 1), 94), (512,), 403, 124954, jnp.int32), jax.random.randint(jax.random.fold_in(jax.random.fold_in(_rk, 1), 95), (512,), 1691, 998869, jnp.int32), jax.random.randint(jax.random.fold_in(jax.random.fold_in(_rk, 1), 96), (512,), 216, 999909, jnp.int32), jax.random.randint(jax.random.fold_in(jax.random.fold_in(_rk, 1), 97), (512,), 279, 999594, jnp.int32), jax.random.randint(jax.random.fold_in(jax.random.fold_in(_rk, 1), 98), (512,), 7628, 997490, jnp.int32), jax.random.randint(jax.random.fold_in(jax.random.fold_in(_rk, 1), 99), (512,), 922, 997835, jnp.int32), jax.random.randint(jax.random.fold_in(jax.random.fold_in(_rk, 1), 100), (512,), 436, 999837, jnp.int32), jax.random.randint(jax.random.fold_in(jax.random.fold_in(_rk, 1), 101), (512,), 1843, 999239, jnp.int32), jax.random.randint(jax.random.fold_in(jax.random.fold_in(_rk, 1), 102), (512,), 974, 998724, jnp.int32), jax.random.randint(jax.random.fold_in(jax.random.fold_in(_rk, 1), 103), (512,), 882, 996710, jnp.int32), jax.random.randint(jax.random.fold_in(jax.random.fold_in(_rk, 1), 104), (512,), 1441, 999983, jnp.int32), jax.random.randint(jax.random.fold_in(jax.random.fold_in(_rk, 1), 105), (512,), 1138, 999340, jnp.int32), jax.random.randint(jax.random.fold_in(jax.random.fold_in(_rk, 1), 106), (512,), 28, 999252, jnp.int32), jax.random.randint(jax.random.fold_in(jax.random.fold_in(_rk, 1), 107), (512,), 2310, 999919, jnp.int32), jax.random.randint(jax.random.fold_in(jax.random.fold_in(_rk, 1), 108), (512,), 200, 999885, jnp.int32), jax.random.randint(jax.random.fold_in(jax.random.fold_in(_rk, 1), 109), (512,), 2226, 124861, jnp.int32), jax.random.randint(jax.random.fold_in(jax.random.fold_in(_rk, 1), 110), (512,), 310, 999463, jnp.int32), jax.random.randint(jax.random.fold_in(jax.random.fold_in(_rk, 1), 111), (512,), 276, 997649, jnp.int32), jax.random.randint(jax.random.fold_in(jax.random.fold_in(_rk, 1), 112), (512,), 714, 999785, jnp.int32), jax.random.randint(jax.random.fold_in(jax.random.fold_in(_rk, 1), 113), (512,), 405, 999226, jnp.int32), jax.random.randint(jax.random.fold_in(jax.random.fold_in(_rk, 1), 114), (512,), 1179, 999045, jnp.int32), jax.random.randint(jax.random.fold_in(jax.random.fold_in(_rk, 1), 115), (512,), 1890, 124943, jnp.int32), jax.random.randint(jax.random.fold_in(jax.random.fold_in(_rk, 1), 116), (512,), 3157, 997413, jnp.int32), jax.random.randint(jax.random.fold_in(jax.random.fold_in(_rk, 1), 117), (512,), 651, 998953, jnp.int32), jax.random.randint(jax.random.fold_in(jax.random.fold_in(_rk, 1), 118), (512,), 136, 998059, jnp.int32), jax.random.randint(jax.random.fold_in(jax.random.fold_in(_rk, 1), 119), (512,), 586, 999365, jnp.int32), jax.random.randint(jax.random.fold_in(jax.random.fold_in(_rk, 1), 120), (512,), 1587, 998231, jnp.int32), jax.random.randint(jax.random.fold_in(jax.random.fold_in(_rk, 1), 121), (512,), 128, 999092, jnp.int32), jax.random.randint(jax.random.fold_in(jax.random.fold_in(_rk, 1), 122), (512,), 503, 999109, jnp.int32), jax.random.randint(jax.random.fold_in(jax.random.fold_in(_rk, 1), 123), (512,), 1415, 997145, jnp.int32), jax.random.randint(jax.random.fold_in(jax.random.fold_in(_rk, 1), 124), (512,), 1460, 998003, jnp.int32), jax.random.randint(jax.random.fold_in(jax.random.fold_in(_rk, 1), 125), (512,), 3324, 999834, jnp.int32), jax.random.randint(jax.random.fold_in(jax.random.fold_in(_rk, 1), 126), (512,), 107, 999588, jnp.int32), jax.random.randint(jax.random.fold_in(jax.random.fold_in(_rk, 1), 127), (512,), 552, 999893, jnp.int32), jax.random.randint(jax.random.fold_in(jax.random.fold_in(_rk, 1), 128), (512,), 697, 999906, jnp.int32), jax.random.randint(jax.random.fold_in(jax.random.fold_in(_rk, 1), 129), (512,), 708, 999631, jnp.int32), jax.random.randint(jax.random.fold_in(jax.random.fold_in(_rk, 1), 130), (512,), 1086, 999571, jnp.int32), jax.random.randint(jax.random.fold_in(jax.random.fold_in(_rk, 1), 131), (512,), 317, 998439, jnp.int32), jax.random.randint(jax.random.fold_in(jax.random.fold_in(_rk, 1), 132), (512,), 384, 124945, jnp.int32), jax.random.randint(jax.random.fold_in(jax.random.fold_in(_rk, 1), 133), (512,), 835, 124898, jnp.int32), jax.random.randint(jax.random.fold_in(jax.random.fold_in(_rk, 1), 134), (512,), 2651, 998811, jnp.int32), jax.random.randint(jax.random.fold_in(jax.random.fold_in(_rk, 1), 135), (512,), 1849, 997073, jnp.int32), jax.random.randint(jax.random.fold_in(jax.random.fold_in(_rk, 1), 136), (512,), 283, 997246, jnp.int32), jax.random.randint(jax.random.fold_in(jax.random.fold_in(_rk, 1), 137), (512,), 950, 999553, jnp.int32), jax.random.randint(jax.random.fold_in(jax.random.fold_in(_rk, 1), 138), (512,), 485, 999726, jnp.int32), jax.random.randint(jax.random.fold_in(jax.random.fold_in(_rk, 1), 139), (512,), 979, 999757, jnp.int32), jax.random.randint(jax.random.fold_in(jax.random.fold_in(_rk, 1), 140), (512,), 1833, 996895, jnp.int32), jax.random.randint(jax.random.fold_in(jax.random.fold_in(_rk, 1), 141), (512,), 331, 998903, jnp.int32), jax.random.randint(jax.random.fold_in(jax.random.fold_in(_rk, 1), 142), (512,), 30, 999422, jnp.int32), jax.random.randint(jax.random.fold_in(jax.random.fold_in(_rk, 1), 143), (512,), 1163, 999839, jnp.int32), jax.random.randint(jax.random.fold_in(jax.random.fold_in(_rk, 1), 144), (512,), 674, 998090, jnp.int32), jax.random.randint(jax.random.fold_in(jax.random.fold_in(_rk, 1), 145), (512,), 21, 999830, jnp.int32), jax.random.randint(jax.random.fold_in(jax.random.fold_in(_rk, 1), 146), (512,), 29, 999567, jnp.int32), jax.random.randint(jax.random.fold_in(jax.random.fold_in(_rk, 1), 147), (512,), 143, 124902, jnp.int32), jax.random.randint(jax.random.fold_in(jax.random.fold_in(_rk, 1), 148), (512,), 878, 124771, jnp.int32), jax.random.randint(jax.random.fold_in(jax.random.fold_in(_rk, 1), 149), (512,), 1369, 998149, jnp.int32), jax.random.randint(jax.random.fold_in(jax.random.fold_in(_rk, 1), 150), (512,), 772, 999457, jnp.int32), jax.random.randint(jax.random.fold_in(jax.random.fold_in(_rk, 1), 151), (512,), 1382, 999420, jnp.int32), jax.random.randint(jax.random.fold_in(jax.random.fold_in(_rk, 1), 152), (512,), 1756, 999653, jnp.int32), jax.random.randint(jax.random.fold_in(jax.random.fold_in(_rk, 1), 153), (512,), 42, 124948, jnp.int32), jax.random.randint(jax.random.fold_in(jax.random.fold_in(_rk, 1), 154), (512,), 1290, 999966, jnp.int32), jax.random.randint(jax.random.fold_in(jax.random.fold_in(_rk, 1), 155), (512,), 158, 998601, jnp.int32), jax.random.randint(jax.random.fold_in(jax.random.fold_in(_rk, 1), 156), (512,), 3, 999023, jnp.int32), jax.random.randint(jax.random.fold_in(jax.random.fold_in(_rk, 1), 157), (512,), 990, 999625, jnp.int32), jax.random.randint(jax.random.fold_in(jax.random.fold_in(_rk, 1), 158), (512,), 1336, 124591, jnp.int32), jax.random.randint(jax.random.fold_in(jax.random.fold_in(_rk, 1), 159), (512,), 220, 999454, jnp.int32), jax.random.randint(jax.random.fold_in(jax.random.fold_in(_rk, 1), 160), (512,), 52, 999301, jnp.int32), jax.random.randint(jax.random.fold_in(jax.random.fold_in(_rk, 1), 161), (512,), 816, 999317, jnp.int32), jax.random.randint(jax.random.fold_in(jax.random.fold_in(_rk, 1), 162), (512,), 1279, 124556, jnp.int32), jax.random.randint(jax.random.fold_in(jax.random.fold_in(_rk, 1), 163), (512,), 62, 999854, jnp.int32), jax.random.randint(jax.random.fold_in(jax.random.fold_in(_rk, 1), 164), (512,), 790, 999686, jnp.int32), jax.random.randint(jax.random.fold_in(jax.random.fold_in(_rk, 1), 165), (512,), 92, 124884, jnp.int32), jax.random.randint(jax.random.fold_in(jax.random.fold_in(_rk, 1), 166), (512,), 343, 998875, jnp.int32), jax.random.randint(jax.random.fold_in(jax.random.fold_in(_rk, 1), 167), (512,), 49, 999881, jnp.int32), jax.random.randint(jax.random.fold_in(jax.random.fold_in(_rk, 1), 168), (512,), 238, 999667, jnp.int32), jax.random.randint(jax.random.fold_in(jax.random.fold_in(_rk, 1), 169), (512,), 290, 999756, jnp.int32), jax.random.randint(jax.random.fold_in(jax.random.fold_in(_rk, 1), 170), (512,), 1290, 999393, jnp.int32), jax.random.randint(jax.random.fold_in(jax.random.fold_in(_rk, 1), 171), (512,), 315, 999267, jnp.int32), jax.random.randint(jax.random.fold_in(jax.random.fold_in(_rk, 1), 172), (512,), 22, 996857, jnp.int32), jax.random.randint(jax.random.fold_in(jax.random.fold_in(_rk, 1), 173), (512,), 3059, 997820, jnp.int32), jax.random.randint(jax.random.fold_in(jax.random.fold_in(_rk, 1), 174), (512,), 39, 124891, jnp.int32), jax.random.randint(jax.random.fold_in(jax.random.fold_in(_rk, 1), 175), (512,), 125, 998612, jnp.int32), jax.random.randint(jax.random.fold_in(jax.random.fold_in(_rk, 1), 176), (512,), 608, 999559, jnp.int32), jax.random.randint(jax.random.fold_in(jax.random.fold_in(_rk, 1), 177), (512,), 23, 998889, jnp.int32), jax.random.randint(jax.random.fold_in(jax.random.fold_in(_rk, 1), 178), (512,), 403, 997812, jnp.int32), jax.random.randint(jax.random.fold_in(jax.random.fold_in(_rk, 1), 179), (512,), 1844, 999550, jnp.int32), jax.random.randint(jax.random.fold_in(jax.random.fold_in(_rk, 1), 180), (512,), 135, 124892, jnp.int32), jax.random.randint(jax.random.fold_in(jax.random.fold_in(_rk, 1), 181), (512,), 2564, 999209, jnp.int32), jax.random.randint(jax.random.fold_in(jax.random.fold_in(_rk, 1), 182), (512,), 255, 999975, jnp.int32), jax.random.randint(jax.random.fold_in(jax.random.fold_in(_rk, 1), 183), (512,), 628, 999374, jnp.int32), jax.random.randint(jax.random.fold_in(jax.random.fold_in(_rk, 1), 184), (512,), 1, 124850, jnp.int32), jax.random.randint(jax.random.fold_in(jax.random.fold_in(_rk, 1), 185), (512,), 328, 998498, jnp.int32), jax.random.randint(jax.random.fold_in(jax.random.fold_in(_rk, 1), 186), (512,), 1330, 997377, jnp.int32), jax.random.randint(jax.random.fold_in(jax.random.fold_in(_rk, 1), 187), (512,), 1134, 999554, jnp.int32), jax.random.randint(jax.random.fold_in(jax.random.fold_in(_rk, 1), 188), (512,), 476, 999035, jnp.int32), jax.random.randint(jax.random.fold_in(jax.random.fold_in(_rk, 1), 189), (512,), 524, 998474, jnp.int32), jax.random.randint(jax.random.fold_in(jax.random.fold_in(_rk, 1), 190), (512,), 275, 124837, jnp.int32), jax.random.randint(jax.random.fold_in(jax.random.fold_in(_rk, 1), 191), (512,), 1334, 999908, jnp.int32), jax.random.randint(jax.random.fold_in(jax.random.fold_in(_rk, 1), 192), (512,), 1969, 996163, jnp.int32), jax.random.randint(jax.random.fold_in(jax.random.fold_in(_rk, 1), 193), (512,), 350, 999957, jnp.int32), jax.random.randint(jax.random.fold_in(jax.random.fold_in(_rk, 1), 194), (512,), 1311, 999318, jnp.int32), jax.random.randint(jax.random.fold_in(jax.random.fold_in(_rk, 1), 195), (512,), 1184, 999834, jnp.int32), jax.random.randint(jax.random.fold_in(jax.random.fold_in(_rk, 1), 196), (512,), 441, 997830, jnp.int32), jax.random.randint(jax.random.fold_in(jax.random.fold_in(_rk, 1), 197), (512,), 64, 999991, jnp.int32), jax.random.randint(jax.random.fold_in(jax.random.fold_in(_rk, 1), 198), (512,), 2437, 999353, jnp.int32), jax.random.randint(jax.random.fold_in(jax.random.fold_in(_rk, 1), 199), (512,), 742, 997924, jnp.int32), jax.random.randint(jax.random.fold_in(jax.random.fold_in(_rk, 1), 200), (512,), 1409, 999098, jnp.int32), jax.random.randint(jax.random.fold_in(jax.random.fold_in(_rk, 1), 201), (512,), 716, 999850, jnp.int32), jax.random.randint(jax.random.fold_in(jax.random.fold_in(_rk, 1), 202), (512,), 1630, 994946, jnp.int32), jax.random.randint(jax.random.fold_in(jax.random.fold_in(_rk, 1), 203), (512,), 194, 999116, jnp.int32), jax.random.randint(jax.random.fold_in(jax.random.fold_in(_rk, 1), 204), (512,), 1226, 998213, jnp.int32), jax.random.randint(jax.random.fold_in(jax.random.fold_in(_rk, 1), 205), (512,), 1456, 999998, jnp.int32), jax.random.randint(jax.random.fold_in(jax.random.fold_in(_rk, 1), 206), (512,), 1473, 999210, jnp.int32), jax.random.randint(jax.random.fold_in(jax.random.fold_in(_rk, 1), 207), (512,), 2468, 999050, jnp.int32), jax.random.randint(jax.random.fold_in(jax.random.fold_in(_rk, 1), 208), (512,), 475, 999604, jnp.int32), jax.random.randint(jax.random.fold_in(jax.random.fold_in(_rk, 1), 209), (512,), 812, 999233, jnp.int32), jax.random.randint(jax.random.fold_in(jax.random.fold_in(_rk, 1), 210), (512,), 58, 999701, jnp.int32), jax.random.randint(jax.random.fold_in(jax.random.fold_in(_rk, 1), 211), (512,), 1682, 124968, jnp.int32), jax.random.randint(jax.random.fold_in(jax.random.fold_in(_rk, 1), 212), (512,), 1943, 999477, jnp.int32), jax.random.randint(jax.random.fold_in(jax.random.fold_in(_rk, 1), 213), (512,), 1731, 999501, jnp.int32), jax.random.randint(jax.random.fold_in(jax.random.fold_in(_rk, 1), 214), (512,), 71, 999513, jnp.int32), jax.random.randint(jax.random.fold_in(jax.random.fold_in(_rk, 1), 215), (512,), 904, 998633, jnp.int32), jax.random.randint(jax.random.fold_in(jax.random.fold_in(_rk, 1), 216), (512,), 764, 999853, jnp.int32), jax.random.randint(jax.random.fold_in(jax.random.fold_in(_rk, 1), 217), (512,), 1226, 999463, jnp.int32), jax.random.randint(jax.random.fold_in(jax.random.fold_in(_rk, 1), 218), (512,), 864, 999642, jnp.int32), jax.random.randint(jax.random.fold_in(jax.random.fold_in(_rk, 1), 219), (512,), 18, 997354, jnp.int32), jax.random.randint(jax.random.fold_in(jax.random.fold_in(_rk, 1), 220), (512,), 575, 999794, jnp.int32), jax.random.randint(jax.random.fold_in(jax.random.fold_in(_rk, 1), 221), (512,), 2178, 997783, jnp.int32), jax.random.randint(jax.random.fold_in(jax.random.fold_in(_rk, 1), 222), (512,), 1399, 998172, jnp.int32), jax.random.randint(jax.random.fold_in(jax.random.fold_in(_rk, 1), 223), (512,), 507, 999732, jnp.int32), jax.random.randint(jax.random.fold_in(jax.random.fold_in(_rk, 1), 224), (512,), 770, 996627, jnp.int32), jax.random.randint(jax.random.fold_in(jax.random.fold_in(_rk, 1), 225), (512,), 39, 999689, jnp.int32), jax.random.randint(jax.random.fold_in(jax.random.fold_in(_rk, 1), 226), (512,), 2047, 996182, jnp.int32), jax.random.randint(jax.random.fold_in(jax.random.fold_in(_rk, 1), 227), (512,), 2393, 999822, jnp.int32), jax.random.randint(jax.random.fold_in(jax.random.fold_in(_rk, 1), 228), (512,), 1095, 995514, jnp.int32), jax.random.randint(jax.random.fold_in(jax.random.fold_in(_rk, 1), 229), (512,), 620, 998845, jnp.int32), jax.random.randint(jax.random.fold_in(jax.random.fold_in(_rk, 1), 230), (512,), 400, 124439, jnp.int32), jax.random.randint(jax.random.fold_in(jax.random.fold_in(_rk, 1), 231), (512,), 946, 999594, jnp.int32), jax.random.randint(jax.random.fold_in(jax.random.fold_in(_rk, 1), 232), (512,), 1230, 124964, jnp.int32), jax.random.randint(jax.random.fold_in(jax.random.fold_in(_rk, 1), 233), (512,), 431, 997171, jnp.int32), jax.random.randint(jax.random.fold_in(jax.random.fold_in(_rk, 1), 234), (512,), 938, 997261, jnp.int32), jax.random.randint(jax.random.fold_in(jax.random.fold_in(_rk, 1), 235), (512,), 1189, 124980, jnp.int32), jax.random.randint(jax.random.fold_in(jax.random.fold_in(_rk, 1), 236), (512,), 287, 999603, jnp.int32), jax.random.randint(jax.random.fold_in(jax.random.fold_in(_rk, 1), 237), (512,), 614, 998262, jnp.int32), jax.random.randint(jax.random.fold_in(jax.random.fold_in(_rk, 1), 238), (512,), 226, 999402, jnp.int32), jax.random.randint(jax.random.fold_in(jax.random.fold_in(_rk, 1), 239), (512,), 991, 999609, jnp.int32), jax.random.randint(jax.random.fold_in(jax.random.fold_in(_rk, 1), 240), (512,), 254, 999303, jnp.int32), jax.random.randint(jax.random.fold_in(jax.random.fold_in(_rk, 1), 241), (512,), 100, 999151, jnp.int32), jax.random.randint(jax.random.fold_in(jax.random.fold_in(_rk, 1), 242), (512,), 1807, 998437, jnp.int32), jax.random.randint(jax.random.fold_in(jax.random.fold_in(_rk, 1), 243), (512,), 510, 999517, jnp.int32), jax.random.randint(jax.random.fold_in(jax.random.fold_in(_rk, 1), 244), (512,), 137, 996819, jnp.int32), jax.random.randint(jax.random.fold_in(jax.random.fold_in(_rk, 1), 245), (512,), 618, 999035, jnp.int32), jax.random.randint(jax.random.fold_in(jax.random.fold_in(_rk, 1), 246), (512,), 144, 998333, jnp.int32), jax.random.randint(jax.random.fold_in(jax.random.fold_in(_rk, 1), 247), (512,), 65, 999543, jnp.int32), jax.random.randint(jax.random.fold_in(jax.random.fold_in(_rk, 1), 248), (512,), 18, 999837, jnp.int32), jax.random.randint(jax.random.fold_in(jax.random.fold_in(_rk, 1), 249), (512,), 186, 999646, jnp.int32), jax.random.randint(jax.random.fold_in(jax.random.fold_in(_rk, 1), 250), (512,), 193, 999903, jnp.int32), jax.random.randint(jax.random.fold_in(jax.random.fold_in(_rk, 1), 251), (512,), 3533, 999812, jnp.int32), jax.random.randint(jax.random.fold_in(jax.random.fold_in(_rk, 1), 252), (512,), 442, 999471, jnp.int32), jax.random.randint(jax.random.fold_in(jax.random.fold_in(_rk, 1), 253), (512,), 2859, 999106, jnp.int32), jax.random.randint(jax.random.fold_in(jax.random.fold_in(_rk, 1), 254), (512,), 158, 999850, jnp.int32), jax.random.randint(jax.random.fold_in(jax.random.fold_in(_rk, 1), 255), (512,), 2281, 998682, jnp.int32)], axis=1)
        r_seq_lens = jax.random.randint(jax.random.fold_in(_rk, 2), (512,), 0, 256, jnp.int32)
        return (r_item_his, r_seq_lens)
    r_item_his, r_seq_lens = _rec_inputs()

    def _L0_rec_setup():
        import jax, jax.numpy as jnp
        from jax import lax
        import numpy as np
        B, T, D, H, N_MID = (1024, 256, 64, 128, 125000)

        def _gru_final_state(x, seq_lens, gate_kernel, gate_bias, cand_kernel, cand_bias):
            b, t, d = x.shape
            h_dim = cand_bias.shape[0]
            mask = jnp.arange(t)[None, :] < seq_lens[:, None]

            def step(h, inp):
                xt, m = inp
                xh = jnp.concatenate([xt, h], axis=-1)
                g = jax.nn.sigmoid(xh @ gate_kernel + gate_bias)
                r, u = jnp.split(g, 2, axis=-1)
                xrh = jnp.concatenate([xt, r * h], axis=-1)
                c = jnp.tanh(xrh @ cand_kernel + cand_bias)
                h_new = u * h + (1.0 - u) * c
                h = jnp.where(m[:, None], h_new, h)
                return (h, None)
            h0 = jnp.zeros((b, h_dim), dtype=x.dtype)
            xs = (jnp.swapaxes(x, 0, 1), jnp.swapaxes(mask, 0, 1))
            hT, _ = lax.scan(step, h0, xs)
            return hT
        key = jax.random.key(seed)
        ks = jax.random.split(key, 7)
        item_his = jax.random.randint(ks[0], (B, T), 0, N_MID)
        seq_lens = jax.random.randint(ks[1], (B,), 0, T)
        embedding = jax.random.normal(ks[2], (N_MID, D), dtype=jnp.float32) * 0.05
        gate_kernel = jax.random.normal(ks[3], (D + H, 2 * H), dtype=jnp.float32) * 0.05
        gate_bias = jax.random.normal(ks[4], (2 * H,), dtype=jnp.float32) * 0.05
        cand_kernel = jax.random.normal(ks[5], (D + H, H), dtype=jnp.float32) * 0.05
        cand_bias = jax.random.normal(ks[6], (H,), dtype=jnp.float32) * 0.05
        return {'item_his': item_his, 'seq_lens': seq_lens, 'embedding': embedding, 'gate_kernel': gate_kernel, 'gate_bias': gate_bias, 'cand_kernel': cand_kernel, 'cand_bias': cand_bias}
    _L0_rec_all = _L0_rec_setup()
    _L0_rec_in = {k: v for k, v in _L0_rec_all.items() if k in ('embedding', 'gate_kernel', 'gate_bias', 'cand_kernel', 'cand_bias')}
    del _L0_rec_all
    return {'r_item_his': r_item_his, 'r_seq_lens': r_seq_lens, 'L0_rec_embedding': _L0_rec_in['embedding'], 'L0_rec_gate_kernel': _L0_rec_in['gate_kernel'], 'L0_rec_gate_bias': _L0_rec_in['gate_bias'], 'L0_rec_cand_kernel': _L0_rec_in['cand_kernel'], 'L0_rec_cand_bias': _L0_rec_in['cand_bias']}

def reference(r_item_his, r_seq_lens, L0_rec_embedding, L0_rec_gate_kernel, L0_rec_gate_bias, L0_rec_cand_kernel, L0_rec_cand_bias):
    import jax
    import jax.numpy as jnp

    def _L0_rec_ref(item_his, seq_lens, embedding, gate_kernel, gate_bias, cand_kernel, cand_bias):
        import jax, jax.numpy as jnp
        from jax import lax
        import numpy as np
        B, T, D, H, N_MID = (1024, 256, 64, 128, 125000)

        def _gru_final_state(x, seq_lens, gate_kernel, gate_bias, cand_kernel, cand_bias):
            b, t, d = x.shape
            h_dim = cand_bias.shape[0]
            mask = jnp.arange(t)[None, :] < seq_lens[:, None]

            def step(h, inp):
                xt, m = inp
                xh = jnp.concatenate([xt, h], axis=-1)
                g = jax.nn.sigmoid(xh @ gate_kernel + gate_bias)
                r, u = jnp.split(g, 2, axis=-1)
                xrh = jnp.concatenate([xt, r * h], axis=-1)
                c = jnp.tanh(xrh @ cand_kernel + cand_bias)
                h_new = u * h + (1.0 - u) * c
                h = jnp.where(m[:, None], h_new, h)
                return (h, None)
            h0 = jnp.zeros((b, h_dim), dtype=x.dtype)
            xs = (jnp.swapaxes(x, 0, 1), jnp.swapaxes(mask, 0, 1))
            hT, _ = lax.scan(step, h0, xs)
            return hT
        x = embedding[item_his]
        user_eb = _gru_final_state(x, seq_lens, gate_kernel, gate_bias, cand_kernel, cand_bias)
        return user_eb
    y = _L0_rec_ref(r_item_his, r_seq_lens, L0_rec_embedding, L0_rec_gate_kernel, L0_rec_gate_bias, L0_rec_cand_kernel, L0_rec_cand_bias)
    return y

_drawn_inputs = setup_inputs


def setup_inputs(seed=0):
    import zlib

    import numpy as np

    out = dict(_drawn_inputs(seed))
    spreads = {}
    factors = {'L0_rec_gate_kernel': 8.0, 'L0_rec_gate_bias': 7.411}
    for name, (base, spread) in spreads.items():
        noise = np.random.default_rng([zlib.crc32(name.encode()), seed]).standard_normal(out[name].shape)
        drawn = base * np.exp(spread * noise) if base else spread * noise
        out[name] = jnp.asarray(drawn.astype(out[name].dtype))
    for name, factor in factors.items():
        out[name] = (out[name] * factor).astype(out[name].dtype)
    return out
```

```python
import concourse.bass as bass
from concourse import mybir
from contextlib import ExitStack

F32 = mybir.dt.float32
F32R = mybir.dt.float32r
BF16 = mybir.dt.bfloat16
I32 = mybir.dt.int32
ALU = mybir.AluOpType
ACT = mybir.ActivationFunctionType
AX = mybir.AxisListType

P = 128
LANES = 2
HALF_STEPS = 2
QUAD_STEPS = 2 * HALF_STEPS
COLS = HALF_STEPS * LANES * P
HOLD = 2.0 ** 100


def gru_kernel(nc, item_his, seq_lens, embedding, gate_kernel, gate_bias, cand_kernel, cand_bias, out):
    B, T = item_his.shape
    N_ITEMS, D = embedding.shape
    H = cand_bias.shape[0]
    GROUPS = B // P
    assert GROUPS == 4 and H == P and 2 * D == P
    STEPS = 2 * T + 2 * QUAD_STEPS
    MASK_BLOCKS = -(-STEPS // P)
    REC = T + 2
    MAX_QUADS = 2 * T // QUAD_STEPS

    sorted_dram = nc.dram_tensor("sorted_dram", [B, REC], I32, kind="Internal").ap()
    ended_dram = nc.dram_tensor("ended_dram", [MASK_BLOCKS * P, LANES * P], BF16, kind="Internal").ap()

    ctx = ExitStack()
    with ctx:
        def sb(name, shape, dt):
            return ctx.enter_context(nc.sbuf_tensor(name, shape, dt))

        def pb(name):
            return ctx.enter_context(nc.psum_tensor(name, [P, COLS], F32))

        def sem(name):
            return ctx.enter_context(nc.semaphore(name))

        len_row_i = sb("len_row_i", [P, B], I32)
        key_row = sb("key_row", [P, B], F32)
        number_row = sb("number_row", [P, B], F32)
        records = sb("records", [P, GROUPS, REC], I32)
        wrap = sb("wrap", [P, GROUPS, T], F32)
        number_col = sb("number_col", [P, GROUPS], F32)
        key_col = sb("key_col", [P, GROUPS], F32)
        above = sb("above", [P, B], F32)
        rank_f = sb("rank_f", [P, GROUPS], F32)
        rank_i = sb("rank_i", [P, GROUPS], I32)
        ranked = sb("ranked", [P, GROUPS, REC], I32)
        items = sb("items", [P, STEPS, LANES], I32)
        len_f = sb("len_f", [P, GROUPS], F32)
        diag = sb("diag", [P, GROUPS, P], F32)
        ones = sb("ones", [P, P], F32)
        ident = sb("ident", [P, P], F32)
        longest = sb("longest", [P, GROUPS], F32)
        quads_i = sb("quads_i", [P, GROUPS], I32)
        quads_s = sb("quads_s", [P, GROUPS], I32)
        quads_f = sb("quads_f", [P, GROUPS], F32)
        lane_quads = sb("lane_quads", [P, LANES], F32)
        counts = sb("counts", [P, 4], I32)
        turn_f = sb("turn_f", [P, LANES], F32)
        first_len = sb("first_len", [P, LANES, P], F32)
        second_end = sb("second_end", [P, LANES, P], F32)
        turn_row = sb("turn_row", [P, LANES, P], F32)
        step_col = sb("step_col", [P, MASK_BLOCKS], F32)
        in_first = sb("in_first", [P, LANES, P], F32)
        in_second = sb("in_second", [P, LANES, P], F32)
        past_turn = sb("past_turn", [P, LANES, P], F32)
        ended = sb("ended", [P, MASK_BLOCKS, LANES * P], BF16)
        w_x = sb("w_x", [P, 3 * H], F32)
        w_x_hi = sb("w_x_hi", [P, 3 * H], F32R)
        w_x_lo = sb("w_x_lo", [P, 3 * H], F32R)
        w_h = sb("w_h", [P, 3 * H], F32)
        bias_row = sb("bias_row", [1, 3 * H], F32)
        bias_rest = sb("bias_rest", [1, 2, 3 * H], F32)
        bias_part = sb("bias_part", [1, 4, 3 * H], BF16)
        bias_w = sb("bias_w", [4, 3 * H], BF16)
        item_now = [sb(f"item_now{j}", [P, 4], I32) for j in range(2)]
        x_raw = [sb(f"x_raw{j}", [P, 4, D], F32) for j in range(2)]
        x_split = [sb(f"x_split{j}", [P, 4, 2, D], F32) for j in range(2)]
        x_parts = [sb(f"x_parts{j}", [P, COLS], F32R) for j in range(2)]
        aux = [sb(f"aux{j}", [4, COLS], BF16) for j in range(2)]
        h = [sb(f"h{l}", [P, P], F32) for l in range(LANES)]
        r_gate = [sb(f"r_gate{l}", [P, P], F32) for l in range(LANES)]
        u_gate = [sb(f"u_gate{l}", [P, P], F32) for l in range(LANES)]
        rh = [sb(f"rh{l}", [P, P], F32) for l in range(LANES)]
        fresh = [sb(f"fresh{l}", [P, P], F32) for l in range(LANES)]
        kept = [sb(f"kept{l}", [P, P], F32) for l in range(LANES)]
        cand = [sb(f"cand{l}", [P, P], F32) for l in range(LANES)]
        first_final = [sb(f"first_final{l}", [P, P], F32) for l in range(LANES)]
        final_rows = sb("final_rows", [P, GROUPS, H], F32)

        RC = [[pb(f"RC{l}{j}") for j in range(2)] for l in range(LANES)]
        U = [pb(f"U{l}") for l in range(LANES)]
        xT = [pb(f"xT{j}") for j in range(2)]

        s_in_len = sem("in_len")
        s_in_his = sem("in_his")
        s_in_w = sem("in_w")
        s_in_bias = sem("in_bias")
        s_bias_rows = sem("bias_rows")
        s_const = sem("const")
        s_pool = sem("pool_chain")
        s_dve = sem("dve_chain")
        s_weights = sem("weights_ready")
        s_rank = sem("rank_ready")
        s_scattered = sem("scattered")
        s_ranked = sem("ranked_landed")
        s_diag = sem("diag_ready")
        s_lens = sem("lens_spread")
        s_counts = sem("counts_ready")
        s_items = sem("items_ready")
        s_ended = sem("ended_ready")
        s_ended_out = sem("ended_stored")
        s_aux = sem("aux_ready")
        s_item_now = sem("item_now_ready")
        s_item_seen = sem("item_now_seen")
        s_x = [sem(f"x_landed{j}") for j in range(2)]
        s_end = [sem(f"ended_landed{j}") for j in range(2)]
        s_xT = sem("xT_ready")
        s_hi = sem("hi_ready")
        s_lo = sem("lo_ready")
        s_parts = sem("x_parts_ready")
        s_xu = sem("x_update_done")
        s_h = [sem(f"h_ready{l}") for l in range(LANES)]
        s_rpre = [sem(f"r_pre{l}") for l in range(LANES)]
        s_upre = [sem(f"u_pre{l}") for l in range(LANES)]
        s_cpre = [sem(f"c_pre{l}") for l in range(LANES)]
        s_r = [sem(f"r_gate{l}") for l in range(LANES)]
        s_u = [sem(f"u_gate{l}") for l in range(LANES)]
        s_c = [sem(f"c_ready{l}") for l in range(LANES)]
        s_rh = [sem(f"rh_ready{l}") for l in range(LANES)]
        s_blend = [sem(f"blend_ready{l}") for l in range(LANES)]
        s_final = sem("final_transposed")
        s_rows = sem("final_rows_ready")
        s_out = sem("out_stored")
        s_loads_over = sem("loads_over")

        block = ctx.enter_context(nc.Block())

        def pair(lane):
            return slice(lane * HALF_STEPS * P, (lane + 1) * HALF_STEPS * P)

        def r_col(step):
            return slice(step * P, (step + 1) * P)

        def c_col(step):
            return r_col(HALF_STEPS + step)

        def quads(eng):
            eng.wait_ge(s_counts, 1)
            return eng.value_load(counts[0:1, 2:3], min_val=1, max_val=MAX_QUADS)

        @block.sync
        def _(sp):
            lens_1 = seq_lens.rearrange("(o b) -> o b", o=1)
            sp.dma_start(len_row_i[:, :], lens_1.to_broadcast([P, B])).then_inc(s_in_len, 16)
            sp.dma_start(records[:, :, T], seq_lens.rearrange("(p g) -> p g", g=GROUPS),
                         allow_slow_non_contiguous=True).then_inc(s_in_len, 16)
            sp.dma_start(records[:, :, 0:T], item_his.rearrange("(p g) t -> p g t", g=GROUPS)).then_inc(s_in_his, 16)
            for half in range(2):
                rows = slice(half * D, half * D + D)
                sp.dma_start(w_x[rows, 0:2 * H], gate_kernel[0:D, :]).then_inc(s_in_w, 16)
                sp.dma_start(w_x[rows, 2 * H:3 * H], cand_kernel[0:D, :]).then_inc(s_in_w, 16)
            sp.dma_start(w_h[:, 0:2 * H], gate_kernel[D:D + H, :]).then_inc(s_in_w, 16)
            sp.dma_start(w_h[:, 2 * H:3 * H], cand_kernel[D:D + H, :]).then_inc(s_in_w, 16)
            sp.dma_start(bias_row[:, 0:2 * H], gate_bias.rearrange("(o b) -> o b", o=1)).then_inc(s_in_bias, 16)
            sp.dma_start(bias_row[:, 2 * H:3 * H], cand_bias.rearrange("(o b) -> o b", o=1)).then_inc(s_in_bias, 16)
            sp.wait_ge(s_weights, 2)
            for row in range(4):
                sp.dma_start(bias_w[row:row + 1, :], bias_part[0:1, row, :]).then_inc(s_bias_rows, 16)
            sp.wait_ge(s_scattered, 16 * GROUPS)
            sp.dma_start(ranked[:, :, :], sorted_dram.rearrange("(g p) c -> p g c", p=P)).then_inc(s_ranked, 16)
            for blk in range(MASK_BLOCKS):
                sp.wait_ge(s_ended, blk + 1)
                sp.dma_start(ended_dram[blk * P:(blk + 1) * P, :], ended[:, blk, :]).then_inc(s_ended_out, 16)
            sp.wait_ge(s_ended_out, 16 * MASK_BLOCKS)
            n = quads(sp)

            def load_ended(j, first_step):
                for l in range(LANES):
                    rows = ended_dram[bass.ds(first_step, HALF_STEPS), l * P:(l + 1) * P]
                    sp.dma_start(aux[j][3:4, pair(l)].rearrange("o (s b) -> o s b", b=P),
                                 rows.unsqueeze(0)).then_inc(s_end[j], 16)

            sp.wait_ge(s_aux, 1)
            load_ended(0, 0)
            load_ended(1, HALF_STEPS)
            with sp.Fori(0, n) as q:
                for j in range(2):
                    sp.wait_ge(s_xu, 2 * q + j + 1)
                    load_ended(j, q * QUAD_STEPS + QUAD_STEPS + j * HALF_STEPS)
            sp.wait_ge(s_end[0], 32 * n + 32)
            sp.wait_ge(s_end[1], 32 * n + 32)
            sp.sem_inc(s_loads_over, 1)

        @block.gpsimd
        def _(pool):
            nc.gpsimd.iota(number_row[:, :], pattern=[[1, B]], base=0, channel_multiplier=0,
                           allow_small_or_imprecise_dtypes=True).then_inc(s_const, 1)
            nc.gpsimd.iota(number_col[:, :], pattern=[[1, GROUPS]], base=0, channel_multiplier=GROUPS,
                           allow_small_or_imprecise_dtypes=True).then_inc(s_const, 1)
            nc.gpsimd.iota(records[:, :, T + 1], pattern=[[1, GROUPS]], base=0,
                           channel_multiplier=GROUPS).then_inc(s_const, 1)
            nc.gpsimd.memset(ident[:, :], 0.0).then_inc(s_pool, 1)
            pool.wait_ge(s_pool, 1)
            nc.gpsimd.affine_select(out=ident[:, :], in_=ident[:, :], compare_op=ALU.not_equal, fill=1.0,
                                    base=0, pattern=[[-1, P]], channel_multiplier=1).then_inc(s_const, 1)
            nc.gpsimd.memset(ones[:, :], 1.0).then_inc(s_const, 1)
            nc.gpsimd.iota(step_col[:, :], pattern=[[P, MASK_BLOCKS]], base=0, channel_multiplier=1,
                           allow_small_or_imprecise_dtypes=True).then_inc(s_const, 1)
            for j in range(2):
                last = nc.gpsimd.memset(aux[j][:, :], 1.0)
            last.then_inc(s_aux, 1)
            pool.wait_ge(s_rank, 1)
            for g in range(GROUPS):
                pool.indirect_dma_start(sorted_dram[:, :], bass.IndirectOffsetOnAxis(rank_i[:, g:g + 1], 0),
                                        records[:, g, :], None).then_inc(s_scattered, 16)
            pool.wait_ge(s_items, 1)
            n = quads(pool)

            def gather(j, k, first_step):
                now = nc.gpsimd.tensor_copy(item_now[j][:, :].rearrange("p (l s) -> p s l", l=LANES),
                                            items[:, bass.ds(first_step, HALF_STEPS), :])
                now.then_inc(s_item_now, 1)
                pool.wait_ge(s_item_now, k + 1)
                pool.sem_inc(s_item_seen, 1)
                for c in range(4):
                    pool.indirect_dma_start(x_raw[j][:, c, :], None, embedding[:, :],
                                            bass.IndirectOffsetOnAxis(item_now[j][:, c:c + 1], 0)).then_inc(s_x[j], 16)

            gather(0, 0, 0)
            gather(1, 1, HALF_STEPS)
            pool.wait_ge(s_lo, 1)
            gather(0, 2, 2 * HALF_STEPS)
            with pool.Fori(0, n) as q:
                for j in range(2):
                    pool.wait_ge(s_lo, 2 * q + j + 2)
                    gather(1 - j, 2 * q + j + 3, q * QUAD_STEPS + (j + 3) * HALF_STEPS)

            for g in range(GROUPS):
                pool.wait_ge(s_rows, g + 1)
                pool.indirect_dma_start(out[:, :], bass.IndirectOffsetOnAxis(ranked[:, g, T + 1:T + 2], 0),
                                        final_rows[:, g, :], None).then_inc(s_out, 16)
            pool.wait_ge(s_out, 16 * GROUPS)

        @block.tensor
        def _(pe):
            pe.wait_ge(s_diag, GROUPS)
            for g in range(GROUPS):
                last = nc.tensor.matmul(xT[1][:, g * P:(g + 1) * P], ones[:, :], diag[:, g, :], start=True, stop=True)
            last.then_inc(s_lens, 1)
            pe.wait_ge(s_bias_rows, 64)
            pe.wait_ge(s_weights, 1)
            n = quads(pe)

            def transposes(j, k):
                pe.wait_ge(s_lo, k + 1)
                for c in range(4):
                    rows = x_split[j][:, c, :, :].rearrange("b t d -> b (t d)")
                    last = nc.tensor.transpose(xT[j][:, c * P:(c + 1) * P], rows, ident[:, :])
                last.then_inc(s_xT, 1)

            def x_side(out_cols, gate, lane, j, start):
                w = slice(gate * H, (gate + 1) * H)
                nc.tensor.matmul(out_cols, w_x_hi[:, w], x_parts[j][:, pair(lane)], start=start, stop=False,
                                 skip_group_check=True)
                nc.tensor.matmul(out_cols, w_x_lo[:, w], x_parts[j][:, pair(lane)], start=False, stop=False,
                                 skip_group_check=True)
                return nc.tensor.matmul(out_cols, bias_w[:, w], aux[j][:, pair(lane)], start=False, stop=False,
                                        skip_group_check=True)

            def x_reset(j, lane):
                return x_side(RC[lane][j][:, 0:HALF_STEPS * P], 0, lane, j, True)

            def x_candidate(j, lane):
                return x_side(RC[lane][j][:, HALF_STEPS * P:], 2, lane, j, False)

            def x_update(j, lane):
                return x_side(U[lane][:, 0:HALF_STEPS * P], 1, lane, j, True)

            def x_wait(j, k, ended_landed):
                pe.wait_ge(s_parts, k + 1)
                pe.wait_ge(s_end[j], ended_landed)

            def recur(out_cols, gate, operand):
                w = slice(gate * H, (gate + 1) * H)
                return nc.tensor.matmul(out_cols, w_h[:, w], operand, start=False, stop=True, skip_group_check=True)

            def reset(j, step, lane, s):
                pe.wait_ge(s_h[lane], s + 1)
                recur(RC[lane][j][:, r_col(step)], 0, h[lane][:, :]).then_inc(s_rpre[lane], 1)

            def update(step, lane):
                recur(U[lane][:, r_col(step)], 1, h[lane][:, :]).then_inc(s_upre[lane], 1)

            def candidate(j, step, lane, s):
                pe.wait_ge(s_rh[lane], s + 1)
                recur(RC[lane][j][:, c_col(step)], 2, rh[lane][:, :]).then_inc(s_cpre[lane], 1)

            transposes(0, 0)
            transposes(1, 1)
            x_wait(0, 0, 32)
            for l in range(LANES):
                x_reset(0, l)
                x_candidate(0, l)

            with pe.Fori(0, n) as q:
                for j in range(2):
                    i = 1 - j
                    k = 2 * q + j
                    s = q * QUAD_STEPS + j * HALF_STEPS
                    reset(j, 0, 0, s)
                    reset(j, 0, 1, s)
                    x_update(j, 0)
                    update(0, 0)
                    x_update(j, 1).then_inc(s_xu, 1)
                    update(0, 1)
                    candidate(j, 0, 0, s)
                    candidate(j, 0, 1, s)
                    transposes(j, k + 2)
                    x_wait(i, k + 1, (q + j + 1) * 32)
                    x_reset(i, 0)
                    reset(j, 1, 0, s + 1)
                    reset(j, 1, 1, s + 1)
                    update(1, 0)
                    update(1, 1)
                    x_candidate(i, 0)
                    candidate(j, 1, 0, s + 1)
                    candidate(j, 1, 1, s + 1)
                    x_reset(i, 1)
                    x_candidate(i, 1)

            for l in range(LANES):
                pe.wait_ge(s_h[l], n * QUAD_STEPS + 1)
            for g, state in enumerate((first_final[0], first_final[1], h[1], h[0])):
                nc.tensor.transpose(xT[1][:, g * P:(g + 1) * P], state[:, :], ident[:, :]).then_inc(s_final, 1)

        @block.scalar
        def _(act):
            def high_part(j, k, landed, transposed):
                act.wait_ge(s_x[j], landed)
                act.wait_ge(s_xT, transposed)
                nc.scalar.copy(x_split[j][:, :, 0, :].bitcast(F32R), x_raw[j][:, :, :]).then_inc(s_hi, 1)

            def reset(j, step, lane, s):
                act.wait_ge(s_rpre[lane], s + 1)
                nc.scalar.activation(r_gate[lane][:, :], RC[lane][j][:, r_col(step)], ACT.Sigmoid).then_inc(s_r[lane], 1)

            def update(step, lane, s):
                act.wait_ge(s_upre[lane], s + 1)
                nc.scalar.activation(u_gate[lane][:, :], U[lane][:, r_col(step)], ACT.Sigmoid).then_inc(s_u[lane], 1)

            def candidate(j, step, lane, s):
                act.wait_ge(s_cpre[lane], s + 1)
                nc.scalar.activation(cand[lane][:, :], RC[lane][j][:, c_col(step)], ACT.Tanh).then_inc(s_c[lane], 1)

            n = quads(act)
            high_part(0, 0, 64, 0)
            high_part(1, 1, 64, 0)
            high_part(0, 2, 128, 1)
            with act.Fori(0, n) as q:
                for j in range(2):
                    s = q * QUAD_STEPS + j * HALF_STEPS
                    for step in range(HALF_STEPS):
                        reset(j, step, 0, s + step)
                        reset(j, step, 1, s + step)
                        update(step, 0, s + step)
                        update(step, 1, s + step)
                        if step == 0:
                            high_part(1 - j, 2 * q + j + 3, (q + j + 2) * 64, 2 * q + j + 2)
                        candidate(j, step, 0, s + step)
                        candidate(j, step, 1, s + step)

        @block.vector
        def _(dve):
            chain = [0]

            def link(ins):
                chain[0] += 1
                ins.then_inc(s_dve, 1)
                dve.wait_ge(s_dve, chain[0])

            dve.wait_ge(s_in_len, 32)
            dve.wait_ge(s_const, 3)
            top = float(T)
            for g_len, g_num, key in ((len_row_i[:, :], number_row[:, :], key_row[:, :]),
                                      (records[:, :, T], number_col[:, :], key_col[:, :])):
                link(nc.vector.tensor_scalar(key, g_len, top, 0.0, ALU.min, ALU.max))
                if g_len.shape[1] == GROUPS:
                    link(nc.vector.tensor_copy(records[:, :, T], key))
                link(nc.vector.scalar_tensor_tensor(key, key, float(B), g_num, ALU.mult, ALU.subtract))
            for g in range(GROUPS):
                link(nc.vector.tensor_scalar(above[:, :], key_row[:, :], key_col[:, g:g + 1], None, ALU.is_gt,
                                             ALU.add, accum_out=rank_f[:, g:g + 1]))
            link(nc.vector.tensor_copy(rank_i[:, :], rank_f[:, :]))
            dve.wait_ge(s_in_his, 16)
            his = records[:, :, 0:T]
            link(nc.vector.tensor_scalar(wrap[:, :, :], his, 0.0, float(N_ITEMS), ALU.is_lt, ALU.mult))
            link(nc.vector.tensor_tensor(wrap[:, :, :], wrap[:, :, :], his, ALU.add))
            link(nc.vector.tensor_scalar(his, wrap[:, :, :], 0.0, float(N_ITEMS - 1), ALU.max, ALU.min))
            nc.vector.memset(items[:, :, :].rearrange("p s l -> p (s l)"), 0).then_inc(s_rank, 1)
            dve.wait_ge(s_rank, 1)
            dve.wait_ge(s_in_w, 96)
            link(nc.vector.tensor_copy(w_x_hi[:, :], w_x[:, :]))
            nc.vector.tensor_tensor(w_x_lo[:, :], w_x[:, :], w_x_hi[:, :].bitcast(F32),
                                    ALU.subtract).then_inc(s_weights, 1)
            dve.wait_ge(s_in_bias, 32)
            link(nc.vector.memset(bias_part[0:1, 3, :], 0.0))
            link(nc.vector.memset(bias_part[0:1, 3, H:2 * H], HOLD))
            link(nc.vector.tensor_copy(bias_part[0:1, 0, :], bias_row[:, :]))
            link(nc.vector.tensor_tensor(bias_rest[:, 0, :], bias_row[:, :], bias_part[0:1, 0, :], ALU.subtract))
            link(nc.vector.tensor_copy(bias_part[0:1, 1, :], bias_rest[:, 0, :]))
            link(nc.vector.tensor_tensor(bias_rest[:, 1, :], bias_rest[:, 0, :], bias_part[0:1, 1, :], ALU.subtract))
            nc.vector.tensor_copy(bias_part[0:1, 2, :], bias_rest[:, 1, :]).then_inc(s_weights, 1)
            dve.wait_ge(s_ranked, 16)
            dve.wait_ge(s_const, 6)
            link(nc.vector.tensor_copy(len_f[:, :], ranked[:, :, T]))
            for g in range(GROUPS):
                nc.vector.tensor_scalar(diag[:, g, :], ident[:, :], len_f[:, g:g + 1], None,
                                        ALU.mult).then_inc(s_diag, 1)
            dve.wait_ge(s_lens, 1)
            lens = xT[1][:, :].rearrange("p (g b) -> p g b", g=GROUPS)
            link(nc.vector.reduce_max(longest[:, :], lens, AX.X))
            link(nc.vector.tensor_scalar(quads_i[:, :], longest[:, :], float(QUAD_STEPS - 1), None, ALU.add))
            link(nc.vector.tensor_scalar(quads_s[:, :], quads_i[:, :], QUAD_STEPS.bit_length() - 1, None,
                                         ALU.logical_shift_right))
            link(nc.vector.tensor_scalar(quads_f[:, :], quads_s[:, :], 1.0, None, ALU.max))
            for l in range(LANES):
                link(nc.vector.tensor_tensor(lane_quads[:, l:l + 1], quads_f[:, l:l + 1],
                                             quads_f[:, GROUPS - 1 - l:GROUPS - l], ALU.add))
            link(nc.vector.tensor_copy(counts[:, 0:2], quads_f[:, 0:2]))
            nc.vector.tensor_tensor(counts[:, 2:3], lane_quads[:, 0:1], lane_quads[:, 1:2], ALU.max).then_inc(s_counts, 1)
            dve.wait_ge(s_counts, 1)
            n_first = [dve.value_load(counts[0:1, l:l + 1], min_val=1, max_val=T // QUAD_STEPS) for l in range(LANES)]
            n = quads(dve)
            for l in range(LANES):
                link(nc.vector.tensor_copy(items[:, 0:T, l], ranked[:, l, 0:T]))
                last = nc.vector.tensor_copy(items[:, bass.ds(n_first[l] * QUAD_STEPS, T), l], ranked[:, GROUPS - 1 - l, 0:T])
                link(last)
            link(nc.vector.tensor_scalar(turn_f[:, :], quads_f[:, 0:LANES], float(QUAD_STEPS), None, ALU.mult))
            nc.vector.memset(h[0][:, :], 0.0).then_inc(s_items, 1)
            for l in range(LANES):
                link(nc.vector.tensor_copy(first_len[:, l, :], lens[:, l, :]))
                link(nc.vector.tensor_scalar(turn_row[:, l, :], ones[:, :], turn_f[:, l:l + 1], None, ALU.mult))
                link(nc.vector.tensor_tensor(second_end[:, l, :], lens[:, GROUPS - 1 - l, :], turn_row[:, l, :], ALU.add))
            for blk in range(MASK_BLOCKS):
                now = step_col[:, blk:blk + 1]
                link(nc.vector.tensor_scalar(in_first[:, :, :], first_len[:, :, :], now, None, ALU.is_gt))
                link(nc.vector.tensor_scalar(in_second[:, :, :], second_end[:, :, :], now, None, ALU.is_gt))
                link(nc.vector.tensor_scalar(past_turn[:, :, :], turn_row[:, :, :], now, None, ALU.is_le))
                link(nc.vector.tensor_tensor(in_second[:, :, :], in_second[:, :, :], past_turn[:, :, :], ALU.mult))
                link(nc.vector.tensor_tensor(in_first[:, :, :], in_first[:, :, :], in_second[:, :, :], ALU.add))
                nc.vector.tensor_scalar(ended[:, blk, :].rearrange("p (l b) -> p l b", l=LANES), in_first[:, :, :],
                                        0.5, None, ALU.is_lt).then_inc(s_ended, 1)
                dve.wait_ge(s_ended, blk + 1)
            dve.wait_ge(s_items, 1)
            nc.vector.memset(h[1][:, :], 0.0).then_inc(s_h[1], 1)
            dve.sem_inc(s_h[0], 1)

            def low_part(j, k):
                dve.wait_ge(s_hi, k + 1)
                nc.vector.tensor_tensor(x_split[j][:, :, 1, :], x_raw[j][:, :, :], x_split[j][:, :, 0, :],
                                        ALU.subtract).then_inc(s_lo, 1)

            def operand(j, k):
                dve.wait_ge(s_xT, k + 1)
                nc.vector.tensor_copy(x_parts[j][:, :], xT[j][:, :]).then_inc(s_parts, 1)

            def reset(lane, s):
                dve.wait_ge(s_r[lane], s + 1)
                nc.vector.tensor_tensor(rh[lane][:, :], r_gate[lane][:, :], h[lane][:, :],
                                        ALU.mult).then_inc(s_rh[lane], 1)

            def keep(lane, s):
                dve.wait_ge(s_u[lane], s + 1)
                nc.vector.tensor_tensor(kept[lane][:, :], u_gate[lane][:, :], h[lane][:, :],
                                        ALU.mult).then_inc(s_blend[lane], 1)

            def blend(lane, s):
                dve.wait_ge(s_c[lane], s + 1)
                nc.vector.scalar_tensor_tensor(fresh[lane][:, :], u_gate[lane][:, :], 1.0, cand[lane][:, :],
                                               ALU.subtract, ALU.mult).then_inc(s_blend[lane], 1)
                dve.wait_ge(s_blend[lane], 2 * s + 2)

            def new_state(to, lane):
                return nc.vector.tensor_tensor(to[:, :], kept[lane][:, :], fresh[lane][:, :], ALU.subtract)

            low_part(0, 0)
            low_part(1, 1)
            low_part(0, 2)
            operand(0, 0)
            operand(1, 1)
            with dve.Fori(0, n) as q:
                for j in range(2):
                    s = q * QUAD_STEPS + j * HALF_STEPS
                    for step in range(HALF_STEPS):
                        reset(0, s + step)
                        reset(1, s + step)
                        keep(0, s + step)
                        keep(1, s + step)
                        if step == 0:
                            low_part(1 - j, 2 * q + j + 3)
                        else:
                            operand(j, 2 * q + j + 2)
                        for lane in range(LANES):
                            blend(lane, s + step)
                            if j == 1 and step == HALF_STEPS - 1:
                                with dve.If(q == n_first[lane] - 1):
                                    new_state(first_final[lane], lane)
                                    nc.vector.memset(h[lane][:, :], 0.0).then_inc(s_h[lane], 1)
                                with dve.Else():
                                    new_state(h[lane], lane).then_inc(s_h[lane], 1)
                            else:
                                new_state(h[lane], lane).then_inc(s_h[lane], 1)
            dve.wait_ge(s_final, GROUPS)
            for g in range(GROUPS):
                nc.vector.tensor_copy(final_rows[:, g, :], xT[1][:, g * P:(g + 1) * P]).then_inc(s_rows, 1)


_INS = ["r_item_his", "r_seq_lens", "L0_rec_embedding", "L0_rec_gate_kernel", "L0_rec_gate_bias",
        "L0_rec_cand_kernel", "L0_rec_cand_bias"]


def kernel(**inputs):
    import numpy as _np
    import concourse.bacc as _bacc
    from concourse import mybir as _mybir
    from concourse.bass_utils import run_bass_kernel_spmd as _run

    nc = _bacc.Bacc("TRN2", target_bir_lowering=False, num_devices=1)
    arrays, args = {}, []
    for name in _INS:
        a = _np.ascontiguousarray(inputs[name])
        arrays[f"in_{name}_dram"] = a
        args.append(nc.dram_tensor(f"in_{name}_dram", a.shape, _mybir.dt.from_np(a.dtype), kind="ExternalInput").ap())
    shape = (inputs["r_item_his"].shape[0], inputs["L0_rec_cand_bias"].shape[0])
    args.append(nc.dram_tensor("out_0_dram", shape, _mybir.dt.float32, kind="ExternalOutput").ap())
    gru_kernel(nc, *args)
    r = _run(nc, [arrays], core_ids=[0])
    return r.results[0]["out_0_dram"]
```

```python
import concourse.bass as bass
from concourse import mybir
from contextlib import ExitStack

F32 = mybir.dt.float32
F32R = mybir.dt.float32r
BF16 = mybir.dt.bfloat16
I32 = mybir.dt.int32
ALU = mybir.AluOpType
ACT = mybir.ActivationFunctionType
AX = mybir.AxisListType

P = 128
LANES = 2
HALF_STEPS = 2
QUAD_STEPS = 2 * HALF_STEPS
COLS = HALF_STEPS * LANES * P
HOLD = 2.0 ** 100


def gru_kernel(nc, item_his, seq_lens, embedding, gate_kernel, gate_bias, cand_kernel, cand_bias, out):
    B, T = item_his.shape
    N_ITEMS, D = embedding.shape
    H = cand_bias.shape[0]
    GROUPS = B // P
    assert GROUPS == 4 and H == P and 2 * D == P
    STEPS = 2 * T + 4 * QUAD_STEPS
    MASK_BLOCKS = -(-STEPS // P)
    REC = T + 2
    MAX_TURN = T // QUAD_STEPS + 1
    MAX_QUADS = MAX_TURN + T // QUAD_STEPS
    TURN_BITS = MAX_TURN.bit_length()
    QUAD_SHIFT = QUAD_STEPS.bit_length() - 1
    TURN_BLOCKS = -(-(MAX_QUADS + 2) // P)

    sorted_dram = nc.dram_tensor("sorted_dram", [B, REC], I32, kind="Internal").ap()
    ended_dram = nc.dram_tensor("ended_dram", [MASK_BLOCKS * P, LANES * P], BF16, kind="Internal").ap()

    turn_dram = nc.dram_tensor("turn_dram", [TURN_BLOCKS * P, LANES * P], I32, kind="Internal").ap()

    ctx = ExitStack()
    with ctx:
        def sb(name, shape, dt):
            return ctx.enter_context(nc.sbuf_tensor(name, shape, dt))

        def pb(name):
            return ctx.enter_context(nc.psum_tensor(name, [P, COLS], F32))

        def sem(name):
            return ctx.enter_context(nc.semaphore(name))

        len_row_i = sb("len_row_i", [P, B], I32)
        key_row = sb("key_row", [P, B], F32)
        number_row = sb("number_row", [P, B], F32)
        records = sb("records", [P, GROUPS, REC], I32)
        wrap = sb("wrap", [P, GROUPS, T], F32)
        number_col = sb("number_col", [P, GROUPS], F32)
        key_col = sb("key_col", [P, GROUPS], F32)
        above = sb("above", [P, B], F32)
        rank_f = sb("rank_f", [P, GROUPS], F32)
        rank_i = sb("rank_i", [P, GROUPS], I32)
        ranked = sb("ranked", [P, GROUPS, REC], I32)
        items = sb("items", [P, LANES, STEPS], I32)
        shifted = sb("shifted", [P, LANES, STEPS], I32)
        turn_col = sb("turn_col", [P, LANES], I32)
        turn_col_1 = sb("turn_col_1", [P, LANES], I32)
        turn_col_f = sb("turn_col_f", [P, LANES], F32)
        turn_bits = sb("turn_bits", [P, TURN_BITS, LANES], I32)
        before_turn = sb("before_turn", [P, LANES, T], I32)
        upper = sb("upper", [P, GROUPS], F32)
        mirror = sb("mirror", [P, GROUPS], F32)
        len_f = sb("len_f", [P, GROUPS], F32)
        diag = sb("diag", [P, GROUPS, P], F32)
        ones = sb("ones", [P, P], F32)
        zeros = sb("zeros", [P, P], F32)
        ident = sb("ident", [P, P], F32)
        len_row = sb("len_row", [P, GROUPS, P], F32)
        len_up = sb("len_up", [P, GROUPS, P], I32)
        quad_row = sb("quad_row", [P, GROUPS, P], I32)
        turn_row = sb("turn_row", [P, LANES, P], F32)
        turn_step = sb("turn_step", [P, LANES, P], F32)
        column_quads = sb("column_quads", [P, LANES, P], F32)
        most = sb("most", [P, 1], F32)
        counts = sb("counts", [P, 1], I32)
        second_end = sb("second_end", [P, LANES, P], F32)
        step_col = sb("step_col", [P, MASK_BLOCKS], F32)
        in_first = sb("in_first", [P, LANES, P], F32)
        in_second = sb("in_second", [P, LANES, P], F32)
        past_turn = sb("past_turn", [P, LANES, P], F32)
        ended = sb("ended", [P, MASK_BLOCKS, LANES * P], BF16)
        turns = sb("turns", [P, TURN_BLOCKS, LANES * P], I32)
        w_x = sb("w_x", [P, 3 * H], F32)
        w_x_hi = sb("w_x_hi", [P, 3 * H], F32R)
        w_x_lo = sb("w_x_lo", [P, 3 * H], F32R)
        w_h = sb("w_h", [P, 3 * H], F32)
        bias_row = sb("bias_row", [1, 3 * H], F32)
        bias_rest = sb("bias_rest", [1, 2, 3 * H], F32)
        bias_part = sb("bias_part", [1, 4, 3 * H], BF16)
        bias_w = sb("bias_w", [4, 3 * H], BF16)
        turn_now = sb("turn_now", [P, LANES, P], I32)
        item_now = [sb(f"item_now{j}", [P, 4], I32) for j in range(2)]
        x_raw = [sb(f"x_raw{j}", [P, 4, D], F32) for j in range(2)]
        x_split = [sb(f"x_split{j}", [P, 4, 2, D], F32) for j in range(2)]
        x_parts = [sb(f"x_parts{j}", [P, COLS], F32R) for j in range(2)]
        aux = [sb(f"aux{j}", [4, COLS], BF16) for j in range(2)]
        h = [sb(f"h{l}", [P, P], F32) for l in range(LANES)]
        r_gate = [sb(f"r_gate{l}", [P, P], F32) for l in range(LANES)]
        u_gate = [sb(f"u_gate{l}", [P, P], F32) for l in range(LANES)]
        rh = [sb(f"rh{l}", [P, P], F32) for l in range(LANES)]
        fresh = [sb(f"fresh{l}", [P, P], F32) for l in range(LANES)]
        kept = [sb(f"kept{l}", [P, P], F32) for l in range(LANES)]
        cand = [sb(f"cand{l}", [P, P], F32) for l in range(LANES)]
        first_final = [sb(f"first_final{l}", [P, P], F32) for l in range(LANES)]
        final_rows = sb("final_rows", [P, GROUPS, H], F32)

        RC = [[pb(f"RC{l}{j}") for j in range(2)] for l in range(LANES)]
        U = [pb(f"U{l}") for l in range(LANES)]
        xT = [pb(f"xT{j}") for j in range(2)]

        s_in_len = sem("in_len")
        s_in_his = sem("in_his")
        s_in_w = sem("in_w")
        s_in_bias = sem("in_bias")
        s_bias_rows = sem("bias_rows")
        s_const = sem("const")
        s_pool = sem("pool_chain")
        s_dve = sem("dve_chain")
        s_weights = sem("weights_ready")
        s_rank = sem("rank_ready")
        s_scattered = sem("scattered")
        s_ranked = sem("ranked_landed")
        s_diag = sem("diag_ready")
        s_lens = sem("lens_spread")
        s_counts = sem("counts_ready")
        s_items = sem("items_ready")
        s_ended = sem("ended_ready")
        s_ended_out = sem("ended_stored")
        s_aux = sem("aux_ready")
        s_item_now = sem("item_now_ready")
        s_item_seen = sem("item_now_seen")
        s_x = [sem(f"x_landed{j}") for j in range(2)]
        s_end = [sem(f"ended_landed{j}") for j in range(2)]
        s_xT = sem("xT_ready")
        s_hi = sem("hi_ready")
        s_lo = sem("lo_ready")
        s_parts = sem("x_parts_ready")
        s_xu = sem("x_update_done")
        s_h = [sem(f"h_ready{l}") for l in range(LANES)]
        s_rpre = [sem(f"r_pre{l}") for l in range(LANES)]
        s_upre = [sem(f"u_pre{l}") for l in range(LANES)]
        s_cpre = [sem(f"c_pre{l}") for l in range(LANES)]
        s_r = [sem(f"r_gate{l}") for l in range(LANES)]
        s_u = [sem(f"u_gate{l}") for l in range(LANES)]
        s_c = [sem(f"c_ready{l}") for l in range(LANES)]
        s_rh = [sem(f"rh_ready{l}") for l in range(LANES)]
        s_kept = [sem(f"kept_ready{l}") for l in range(LANES)]
        s_fresh = [sem(f"fresh_ready{l}") for l in range(LANES)]
        s_zeroed = sem("turned_zeroed")
        s_turns = sem("turns_ready")
        s_turns_out = sem("turns_stored")
        s_turn = sem("turn_landed")
        s_turn_seen = sem("turn_seen")
        s_final = sem("final_transposed")
        s_rows = sem("final_rows_ready")
        s_act = sem("act_table")
        s_out = sem("out_stored")
        s_loads_over = sem("loads_over")

        block = ctx.enter_context(nc.Block())

        def pair(lane):
            return slice(lane * HALF_STEPS * P, (lane + 1) * HALF_STEPS * P)

        def r_col(step):
            return slice(step * P, (step + 1) * P)

        def c_col(step):
            return r_col(HALF_STEPS + step)

        def quads(eng):
            eng.wait_ge(s_counts, 1)
            return eng.value_load(counts[0:1, 0:1], min_val=1, max_val=MAX_QUADS)

        @block.sync
        def _(sp):
            lens_1 = seq_lens.rearrange("(o b) -> o b", o=1)
            sp.dma_start(len_row_i[:, :], lens_1.to_broadcast([P, B])).then_inc(s_in_len, 16)
            sp.dma_start(records[:, :, T], seq_lens.rearrange("(p g) -> p g", g=GROUPS),
                         allow_slow_non_contiguous=True).then_inc(s_in_len, 16)
            sp.dma_start(records[:, :, 0:T], item_his.rearrange("(p g) t -> p g t", g=GROUPS)).then_inc(s_in_his, 16)
            for half in range(2):
                rows = slice(half * D, half * D + D)
                sp.dma_start(w_x[rows, 0:2 * H], gate_kernel[0:D, :]).then_inc(s_in_w, 16)
                sp.dma_start(w_x[rows, 2 * H:3 * H], cand_kernel[0:D, :]).then_inc(s_in_w, 16)
            sp.dma_start(w_h[:, 0:2 * H], gate_kernel[D:D + H, :]).then_inc(s_in_w, 16)
            sp.dma_start(w_h[:, 2 * H:3 * H], cand_kernel[D:D + H, :]).then_inc(s_in_w, 16)
            sp.dma_start(bias_row[:, 0:2 * H], gate_bias.rearrange("(o b) -> o b", o=1)).then_inc(s_in_bias, 16)
            sp.dma_start(bias_row[:, 2 * H:3 * H], cand_bias.rearrange("(o b) -> o b", o=1)).then_inc(s_in_bias, 16)
            sp.wait_ge(s_weights, 2)
            for row in range(4):
                sp.dma_start(bias_w[row:row + 1, :], bias_part[0:1, row, :]).then_inc(s_bias_rows, 16)
            sp.wait_ge(s_scattered, 16 * GROUPS)
            sp.dma_start(ranked[:, :, :], sorted_dram.rearrange("(g p) c -> p g c", p=P)).then_inc(s_ranked, 16)
            for blk in range(MASK_BLOCKS):
                sp.wait_ge(s_ended, blk + 1)
                sp.dma_start(ended_dram[blk * P:(blk + 1) * P, :], ended[:, blk, :]).then_inc(s_ended_out, 16)
            sp.wait_ge(s_ended_out, 16 * MASK_BLOCKS)
            for blk in range(TURN_BLOCKS):
                sp.wait_ge(s_turns, blk + 1)
                sp.dma_start(turn_dram[blk * P:(blk + 1) * P, :], turns[:, blk, :]).then_inc(s_turns_out, 16)
            sp.wait_ge(s_turns_out, 16 * TURN_BLOCKS)
            n = quads(sp)

            def load_turn(quad):
                row = turn_dram[bass.ds(quad, 1), :]
                sp.dma_start(turn_now[:, :, :].rearrange("p l b -> p (l b)"),
                             row.to_broadcast([P, LANES * P])).then_inc(s_turn, 16)

            def load_ended(j, first_step):
                rows = ended_dram[bass.ds(first_step, HALF_STEPS), :].rearrange("s (l b) -> l s b", l=LANES)
                sp.dma_start(aux[j][3:4, :].rearrange("o (l s b) -> o l s b", l=LANES, b=P),
                             rows.unsqueeze(0)).then_inc(s_end[j], 16)

            sp.wait_ge(s_aux, 1)
            load_ended(0, 0)
            load_ended(1, HALF_STEPS)
            load_turn(1)
            with sp.Fori(0, n) as q:
                for j in range(2):
                    sp.wait_ge(s_xu, 2 * q + j + 1)
                    load_ended(j, q * QUAD_STEPS + QUAD_STEPS + j * HALF_STEPS)
                sp.wait_ge(s_zeroed, q + 1)
                load_turn(q + 2)
            sp.wait_ge(s_end[0], 16 * n + 16)
            sp.wait_ge(s_end[1], 16 * n + 16)
            sp.wait_ge(s_turn, 16 * n + 16)
            sp.sem_inc(s_loads_over, 1)

        @block.gpsimd
        def _(pool):
            nc.gpsimd.iota(number_row[:, :], pattern=[[1, B]], base=0, channel_multiplier=0,
                           allow_small_or_imprecise_dtypes=True).then_inc(s_const, 1)
            nc.gpsimd.iota(number_col[:, :], pattern=[[1, GROUPS]], base=0, channel_multiplier=GROUPS,
                           allow_small_or_imprecise_dtypes=True).then_inc(s_const, 1)
            nc.gpsimd.iota(records[:, :, T + 1], pattern=[[1, GROUPS]], base=0,
                           channel_multiplier=GROUPS).then_inc(s_const, 1)
            nc.gpsimd.memset(ident[:, :], 0.0).then_inc(s_pool, 1)
            pool.wait_ge(s_pool, 1)
            nc.gpsimd.affine_select(out=ident[:, :], in_=ident[:, :], compare_op=ALU.not_equal, fill=1.0,
                                    base=0, pattern=[[-1, P]], channel_multiplier=1).then_inc(s_const, 1)
            nc.gpsimd.memset(zeros[:, :], 0.0)
            nc.gpsimd.memset(ones[:, :], 1.0).then_inc(s_const, 1)
            nc.gpsimd.iota(step_col[:, :], pattern=[[P, MASK_BLOCKS]], base=0, channel_multiplier=1,
                           allow_small_or_imprecise_dtypes=True).then_inc(s_const, 1)
            for j in range(2):
                last = nc.gpsimd.memset(aux[j][:, :], 1.0)
            last.then_inc(s_aux, 1)
            pool.wait_ge(s_rank, 1)
            for g in range(GROUPS):
                pool.indirect_dma_start(sorted_dram[:, :], bass.IndirectOffsetOnAxis(rank_i[:, g:g + 1], 0),
                                        records[:, g, :], None).then_inc(s_scattered, 16)
            pool.wait_ge(s_items, 1)
            n = quads(pool)

            def gather(j, k, first_step):
                now = nc.gpsimd.tensor_copy(item_now[j][:, :].rearrange("p (l s) -> p l s", l=LANES),
                                            items[:, :, bass.ds(first_step, HALF_STEPS)])
                now.then_inc(s_item_now, 1)
                pool.wait_ge(s_item_now, k + 1)
                pool.sem_inc(s_item_seen, 1)
                for c in range(4):
                    pool.indirect_dma_start(x_raw[j][:, c, :], None, embedding[:, :],
                                            bass.IndirectOffsetOnAxis(item_now[j][:, c:c + 1], 0)).then_inc(s_x[j], 16)

            gather(0, 0, 0)
            gather(1, 1, HALF_STEPS)
            pool.wait_ge(s_lo, 1)
            gather(0, 2, 2 * HALF_STEPS)
            with pool.Fori(0, n) as q:
                for j in range(2):
                    pool.wait_ge(s_lo, 2 * q + j + 2)
                    gather(1 - j, 2 * q + j + 3, q * QUAD_STEPS + (j + 3) * HALF_STEPS)

            for g in range(GROUPS):
                pool.wait_ge(s_rows, g + 1)
                pool.indirect_dma_start(out[:, :], bass.IndirectOffsetOnAxis(ranked[:, g, T + 1:T + 2], 0),
                                        final_rows[:, g, :], None).then_inc(s_out, 16)
            pool.wait_ge(s_out, 16 * GROUPS)

        @block.tensor
        def _(pe):
            pe.wait_ge(s_diag, GROUPS)
            for g in range(GROUPS):
                last = nc.tensor.matmul(xT[1][:, g * P:(g + 1) * P], ones[:, :], diag[:, g, :], start=True, stop=True)
            last.then_inc(s_lens, 1)
            pe.wait_ge(s_bias_rows, 64)
            pe.wait_ge(s_weights, 1)
            n = quads(pe)

            def transposes(j, lane):
                for c in range(lane * HALF_STEPS, (lane + 1) * HALF_STEPS):
                    rows = x_split[j][:, c, :, :].rearrange("b t d -> b (t d)")
                    last = nc.tensor.transpose(xT[j][:, c * P:(c + 1) * P], rows, ident[:, :])
                return last

            def x_side(out_cols, gate, lane, j, start):
                w = slice(gate * H, (gate + 1) * H)
                nc.tensor.matmul(out_cols, w_x_hi[:, w], x_parts[j][:, pair(lane)], start=start, stop=False,
                                 skip_group_check=True)
                nc.tensor.matmul(out_cols, w_x_lo[:, w], x_parts[j][:, pair(lane)], start=False, stop=False,
                                 skip_group_check=True)
                return nc.tensor.matmul(out_cols, bias_w[:, w], aux[j][:, pair(lane)], start=False, stop=False,
                                        skip_group_check=True)

            def x_reset(j, lane):
                return x_side(RC[lane][j][:, 0:HALF_STEPS * P], 0, lane, j, True)

            def x_candidate(j, lane):
                return x_side(RC[lane][j][:, HALF_STEPS * P:], 2, lane, j, False)

            def x_update(j, lane):
                return x_side(U[lane][:, 0:HALF_STEPS * P], 1, lane, j, True)

            def x_wait(j, k, ended_landed):
                pe.wait_ge(s_parts, LANES * k + LANES)
                pe.wait_ge(s_end[j], ended_landed)

            def recur(out_cols, gate, operand):
                w = slice(gate * H, (gate + 1) * H)
                return nc.tensor.matmul(out_cols, w_h[:, w], operand, start=False, stop=True, skip_group_check=True)

            def reset(j, step, lane, s):
                pe.wait_ge(s_h[lane], s + 1)
                recur(RC[lane][j][:, r_col(step)], 0, h[lane][:, :]).then_inc(s_rpre[lane], 1)

            def update(step, lane):
                recur(U[lane][:, r_col(step)], 1, h[lane][:, :]).then_inc(s_upre[lane], 1)

            def candidate(j, step, lane, s):
                pe.wait_ge(s_rh[lane], s + 1)
                recur(RC[lane][j][:, c_col(step)], 2, rh[lane][:, :]).then_inc(s_cpre[lane], 1)

            for k in range(2):
                pe.wait_ge(s_lo, k + 1)
                transposes(k, 0)
                transposes(k, 1).then_inc(s_xT, 1)
            x_wait(0, 0, 16)
            for l in range(LANES):
                x_reset(0, l)
                x_candidate(0, l)
            reset(0, 0, 0, 0)

            with pe.Fori(0, n) as q:
                for j in range(2):
                    i = 1 - j
                    k = 2 * q + j
                    s = q * QUAD_STEPS + j * HALF_STEPS
                    x_update(j, 0)
                    update(0, 0)
                    candidate(j, 0, 0, s)
                    x_wait(i, k + 1, (q + j + 1) * 16)
                    x_reset(i, 0)
                    reset(j, 0, 1, s)
                    x_update(j, 1).then_inc(s_xu, 1)
                    update(0, 1)
                    pe.wait_ge(s_lo, k + 3)
                    transposes(j, 0)
                    reset(j, 1, 0, s + 1)
                    candidate(j, 0, 1, s)
                    update(1, 0)
                    transposes(j, 1).then_inc(s_xT, 1)
                    x_reset(i, 1)
                    candidate(j, 1, 0, s + 1)
                    x_candidate(i, 0)
                    reset(j, 1, 1, s + 1)
                    update(1, 1)
                    x_candidate(i, 1)
                    reset(i, 0, 0, s + 2)
                    candidate(j, 1, 1, s + 1)

            for l in range(LANES):
                pe.wait_ge(s_h[l], n * QUAD_STEPS + 1)
            pe.wait_ge(s_parts, LANES * (2 * n + 2))
            for g, state in enumerate((first_final[0], first_final[1], h[0], h[1])):
                nc.tensor.transpose(xT[1][:, g * P:(g + 1) * P], state[:, :], ident[:, :]).then_inc(s_final, 1)

        @block.scalar
        def _(act):
            def high_part(j, k, landed, transposed):
                act.wait_ge(s_x[j], landed)
                act.wait_ge(s_xT, transposed)
                nc.scalar.copy(x_split[j][:, :, 0, :].bitcast(F32R), x_raw[j][:, :, :]).then_inc(s_hi, 1)

            def operand(j, lane, k):
                act.wait_ge(s_xT, k + 1)
                nc.scalar.copy(x_parts[j][:, pair(lane)], xT[j][:, pair(lane)]).then_inc(s_parts, 1)

            def reset(j, step, lane, s):
                act.wait_ge(s_rpre[lane], s + 1)
                nc.scalar.activation(r_gate[lane][:, :], RC[lane][j][:, r_col(step)], ACT.Sigmoid).then_inc(s_r[lane], 1)

            def update(step, lane, s):
                act.wait_ge(s_upre[lane], s + 1)
                nc.scalar.activation(u_gate[lane][:, :], U[lane][:, r_col(step)], ACT.Sigmoid).then_inc(s_u[lane], 1)

            def candidate(j, step, lane, s):
                act.wait_ge(s_cpre[lane], s + 1)
                nc.scalar.activation(cand[lane][:, :], RC[lane][j][:, c_col(step)], ACT.Tanh).then_inc(s_c[lane], 1)

            act.wait_ge(s_const, 5)
            nc.scalar.activation(r_gate[0][:, 0:1], ones[:, 0:1], ACT.Sigmoid).then_inc(s_act, 1)
            n = quads(act)
            high_part(0, 0, 64, 0)
            high_part(1, 1, 64, 0)
            high_part(0, 2, 128, 1)
            for k in range(2):
                for lane in range(LANES):
                    operand(k, lane, k)
            reset(0, 0, 0, 0)
            with act.Fori(0, n) as q:
                for j in range(2):
                    i = 1 - j
                    k = 2 * q + j
                    s = q * QUAD_STEPS + j * HALF_STEPS
                    update(0, 0, s)
                    candidate(j, 0, 0, s)
                    high_part(i, k + 3, (q + j + 2) * 64, k + 2)
                    reset(j, 0, 1, s)
                    update(0, 1, s)
                    reset(j, 1, 0, s + 1)
                    candidate(j, 0, 1, s)
                    update(1, 0, s + 1)
                    operand(j, 0, k + 2)
                    candidate(j, 1, 0, s + 1)
                    operand(j, 1, k + 2)
                    reset(j, 1, 1, s + 1)
                    update(1, 1, s + 1)
                    reset(i, 0, 0, s + 2)
                    candidate(j, 1, 1, s + 1)

        @block.vector
        def _(dve):
            chain = [0]

            def link(ins):
                chain[0] += 1
                ins.then_inc(s_dve, 1)
                dve.wait_ge(s_dve, chain[0])

            dve.wait_ge(s_in_len, 32)
            dve.wait_ge(s_const, 3)
            top = float(T)
            for g_len, g_num, key in ((len_row_i[:, :], number_row[:, :], key_row[:, :]),
                                      (records[:, :, T], number_col[:, :], key_col[:, :])):
                link(nc.vector.tensor_scalar(key, g_len, top, 0.0, ALU.min, ALU.max))
                if g_len.shape[1] == GROUPS:
                    link(nc.vector.tensor_copy(records[:, :, T], key))
                link(nc.vector.scalar_tensor_tensor(key, key, float(B), g_num, ALU.mult, ALU.subtract))
            for g in range(GROUPS):
                link(nc.vector.tensor_scalar(above[:, :], key_row[:, :], key_col[:, g:g + 1], None, ALU.is_gt,
                                             ALU.add, accum_out=rank_f[:, g:g + 1]))
            link(nc.vector.tensor_scalar(upper[:, :], rank_f[:, :], float(B // 2), None, ALU.is_ge))
            link(nc.vector.tensor_scalar(mirror[:, :], rank_f[:, :], -2.0, float(B + B // 2 - 1), ALU.mult, ALU.add))
            link(nc.vector.tensor_tensor(mirror[:, :], mirror[:, :], upper[:, :], ALU.mult))
            link(nc.vector.tensor_tensor(rank_i[:, :], rank_f[:, :], mirror[:, :], ALU.add))
            dve.wait_ge(s_in_his, 16)
            his = records[:, :, 0:T]
            link(nc.vector.tensor_scalar(wrap[:, :, :], his, 0.0, float(N_ITEMS), ALU.is_lt, ALU.mult))
            link(nc.vector.tensor_tensor(wrap[:, :, :], wrap[:, :, :], his, ALU.add))
            link(nc.vector.tensor_scalar(his, wrap[:, :, :], 0.0, float(N_ITEMS - 1), ALU.max, ALU.min))
            nc.vector.memset(items[:, :, :].rearrange("p l s -> p (l s)"), 0).then_inc(s_rank, 1)
            dve.wait_ge(s_rank, 1)
            dve.wait_ge(s_in_w, 96)
            link(nc.vector.tensor_copy(w_x_hi[:, :], w_x[:, :]))
            nc.vector.tensor_tensor(w_x_lo[:, :], w_x[:, :], w_x_hi[:, :].bitcast(F32),
                                    ALU.subtract).then_inc(s_weights, 1)
            dve.wait_ge(s_in_bias, 32)
            link(nc.vector.memset(bias_part[0:1, 3, :], 0.0))
            link(nc.vector.memset(bias_part[0:1, 3, H:2 * H], HOLD))
            link(nc.vector.tensor_copy(bias_part[0:1, 0, :], bias_row[:, :]))
            link(nc.vector.tensor_tensor(bias_rest[:, 0, :], bias_row[:, :], bias_part[0:1, 0, :], ALU.subtract))
            link(nc.vector.tensor_copy(bias_part[0:1, 1, :], bias_rest[:, 0, :]))
            link(nc.vector.tensor_tensor(bias_rest[:, 1, :], bias_rest[:, 0, :], bias_part[0:1, 1, :], ALU.subtract))
            nc.vector.tensor_copy(bias_part[0:1, 2, :], bias_rest[:, 1, :]).then_inc(s_weights, 1)
            dve.wait_ge(s_ranked, 16)
            dve.wait_ge(s_const, 6)
            link(nc.vector.tensor_copy(len_f[:, :], ranked[:, :, T]))
            for g in range(GROUPS):
                nc.vector.tensor_scalar(diag[:, g, :], ident[:, :], len_f[:, g:g + 1], None,
                                        ALU.mult).then_inc(s_diag, 1)
            link(nc.vector.tensor_scalar(turn_col_1[:, :], ranked[:, 0:LANES, T], QUAD_SHIFT, None,
                                         ALU.logical_shift_right))
            link(nc.vector.tensor_scalar(turn_col[:, :], turn_col_1[:, :], 1.0, None, ALU.add))
            link(nc.vector.tensor_scalar(turn_col_f[:, :], turn_col[:, :], float(QUAD_STEPS), None, ALU.mult))
            for k in range(TURN_BITS):
                link(nc.vector.tensor_scalar(turn_bits[:, k, :], turn_col[:, :], k, 1,
                                             ALU.logical_shift_right, ALU.bitwise_and))
            dve.wait_ge(s_lens, 1)
            link(nc.vector.tensor_copy(len_row[:, :, :], xT[1][:, :].rearrange("p (g b) -> p g b", g=GROUPS)))
            first, second = slice(0, LANES), slice(LANES, 2 * LANES)
            link(nc.vector.tensor_scalar(len_up[:, first, :], len_row[:, first, :], float(QUAD_STEPS), None, ALU.add))
            link(nc.vector.tensor_scalar(len_up[:, second, :], len_row[:, second, :], float(QUAD_STEPS - 1), None, ALU.add))
            link(nc.vector.tensor_scalar(quad_row[:, :, :], len_up[:, :, :], QUAD_SHIFT, None, ALU.logical_shift_right))
            link(nc.vector.tensor_copy(turn_row[:, :, :], quad_row[:, first, :]))
            link(nc.vector.tensor_tensor(column_quads[:, :, :], turn_row[:, :, :], quad_row[:, second, :], ALU.add))
            link(nc.vector.reduce_max(most[:, :], column_quads[:, :, :], AX.XY))
            nc.vector.tensor_copy(counts[:, :], most[:, :]).then_inc(s_counts, 1)
            n = quads(dve)
            to = [shifted, items]
            if TURN_BITS % 2 == 0:
                to.reverse()
            link(nc.vector.memset(to[0][:, :, :].rearrange("p l s -> p (l s)"), 0))
            link(nc.vector.tensor_copy(to[0][:, :, 0:T], ranked[:, second, 0:T]))
            for k in range(TURN_BITS):
                src, dst = to[k % 2], to[1 - k % 2]
                shift = QUAD_STEPS << k
                reach = min(STEPS, T + 2 * shift)
                link(nc.vector.tensor_copy(dst[:, :, 0:STEPS], src[:, :, 0:STEPS]))
                link(nc.vector.copy_predicated(dst[:, :, shift:reach],
                                               turn_bits[:, k, :].unsqueeze(2).to_broadcast([P, LANES, reach - shift]),
                                               src[:, :, 0:reach - shift]))
            for l in range(LANES):
                link(nc.vector.tensor_scalar(before_turn[:, l, :], number_row[:, 0:T], turn_col_f[:, l:l + 1], None, ALU.is_lt))
            nc.vector.copy_predicated(items[:, :, 0:T], before_turn[:, :, :], ranked[:, first, 0:T]).then_inc(s_items, 1)
            link(nc.vector.tensor_scalar(turn_step[:, :, :], turn_row[:, :, :], float(QUAD_STEPS), None, ALU.mult))
            link(nc.vector.tensor_tensor(second_end[:, :, :], len_row[:, second, :], turn_step[:, :, :], ALU.add))
            for blk in range(MASK_BLOCKS):
                now = step_col[:, blk:blk + 1]
                link(nc.vector.tensor_scalar(in_first[:, :, :], len_row[:, first, :], now, None, ALU.is_gt))
                link(nc.vector.tensor_scalar(in_second[:, :, :], second_end[:, :, :], now, None, ALU.is_gt))
                link(nc.vector.tensor_scalar(past_turn[:, :, :], turn_step[:, :, :], now, None, ALU.is_le))
                link(nc.vector.tensor_tensor(in_second[:, :, :], in_second[:, :, :], past_turn[:, :, :], ALU.mult))
                link(nc.vector.tensor_tensor(in_first[:, :, :], in_first[:, :, :], in_second[:, :, :], ALU.add))
                nc.vector.tensor_scalar(ended[:, blk, :].rearrange("p (l b) -> p l b", l=LANES), in_first[:, :, :],
                                        0.5, None, ALU.is_lt).then_inc(s_ended, 1)
                dve.wait_ge(s_ended, blk + 1)
            for blk in range(TURN_BLOCKS):
                nc.vector.tensor_scalar(turns[:, blk, :].rearrange("p (l b) -> p l b", l=LANES), turn_row[:, :, :],
                                        step_col[:, blk:blk + 1], None, ALU.is_equal).then_inc(s_turns, 1)
            for l in range(LANES):
                link(nc.vector.memset(first_final[l][:, :], 0.0))
            for l in range(LANES):
                nc.vector.memset(h[l][:, :], 0.0).then_inc(s_h[l], 1)

            def low_part(j, k):
                dve.wait_ge(s_hi, k + 1)
                nc.vector.tensor_tensor(x_split[j][:, :, 1, :], x_raw[j][:, :, :], x_split[j][:, :, 0, :],
                                        ALU.subtract).then_inc(s_lo, 1)

            def reset(lane, s):
                dve.wait_ge(s_r[lane], s + 1)
                nc.vector.tensor_tensor(rh[lane][:, :], r_gate[lane][:, :], h[lane][:, :],
                                        ALU.mult).then_inc(s_rh[lane], 1)

            def keep(lane, s):
                dve.wait_ge(s_u[lane], s + 1)
                nc.vector.tensor_tensor(kept[lane][:, :], u_gate[lane][:, :], h[lane][:, :],
                                        ALU.mult).then_inc(s_kept[lane], 1)

            def turn(lane, s):
                dve.wait_ge(s_h[lane], s + 1)
                dve.wait_ge(s_kept[lane], s + 1)
                dve.sem_inc(s_turn_seen, 1)
                nc.vector.copy_predicated(first_final[lane][:, :], turn_now[:, lane, :], h[lane][:, :])
                return nc.vector.copy_predicated(kept[lane][:, :], turn_now[:, lane, :], zeros[:, :])

            def blend(lane, s):
                dve.wait_ge(s_c[lane], s + 1)
                nc.vector.scalar_tensor_tensor(fresh[lane][:, :], u_gate[lane][:, :], 1.0, cand[lane][:, :],
                                               ALU.subtract, ALU.mult).then_inc(s_fresh[lane], 1)

            def new_state(lane, s):
                dve.wait_ge(s_fresh[lane], s + 1)
                nc.vector.tensor_tensor(h[lane][:, :], kept[lane][:, :], fresh[lane][:, :],
                                        ALU.subtract).then_inc(s_h[lane], 1)

            low_part(0, 0)
            low_part(1, 1)
            low_part(0, 2)
            reset(0, 0)
            with dve.Fori(0, n) as q:
                for j in range(2):
                    for step in range(HALF_STEPS):
                        s = q * QUAD_STEPS + j * HALF_STEPS + step
                        last = j == 1 and step == HALF_STEPS - 1
                        keep(0, s)
                        if last:
                            dve.wait_ge(s_turn, 16 * q + 16)
                            turn(0, s)
                        blend(0, s)
                        new_state(0, s)
                        reset(1, s)
                        keep(1, s)
                        if last:
                            turn(1, s).then_inc(s_zeroed, 1)
                        if j != step:
                            low_part(1 - j, 2 * q + j + 3)
                        reset(0, s + 1)
                        blend(1, s)
                        new_state(1, s)
            dve.wait_ge(s_final, GROUPS)
            for g in range(GROUPS):
                nc.vector.tensor_copy(final_rows[:, g, :], xT[1][:, g * P:(g + 1) * P]).then_inc(s_rows, 1)


_INS = ["r_item_his", "r_seq_lens", "L0_rec_embedding", "L0_rec_gate_kernel", "L0_rec_gate_bias",
        "L0_rec_cand_kernel", "L0_rec_cand_bias"]


def kernel(**inputs):
    import numpy as _np
    import concourse.bacc as _bacc
    from concourse import mybir as _mybir
    from concourse.bass_utils import run_bass_kernel_spmd as _run

    nc = _bacc.Bacc("TRN2", target_bir_lowering=False, num_devices=1)
    arrays, args = {}, []
    for name in _INS:
        a = _np.ascontiguousarray(inputs[name])
        arrays[f"in_{name}_dram"] = a
        args.append(nc.dram_tensor(f"in_{name}_dram", a.shape, _mybir.dt.from_np(a.dtype), kind="ExternalInput").ap())
    shape = (inputs["r_item_his"].shape[0], inputs["L0_rec_cand_bias"].shape[0])
    args.append(nc.dram_tensor("out_0_dram", shape, _mybir.dt.float32, kind="ExternalOutput").ap())
    gru_kernel(nc, *args)
    r = _run(nc, [arrays], core_ids=[0])
    return r.results[0]["out_0_dram"]
```

```python
import concourse.bass as bass
from concourse import mybir
from contextlib import ExitStack

F32 = mybir.dt.float32
F32R = mybir.dt.float32r
BF16 = mybir.dt.bfloat16
I32 = mybir.dt.int32
ALU = mybir.AluOpType
ACT = mybir.ActivationFunctionType
AX = mybir.AxisListType

P = 128
LANES = 2
HALF_STEPS = 2
QUAD_STEPS = 2 * HALF_STEPS
COLS = HALF_STEPS * LANES * P
HOLD = 2.0 ** 100


def gru_kernel(nc, item_his, seq_lens, embedding, gate_kernel, gate_bias, cand_kernel, cand_bias, out):
    B, T = item_his.shape
    N_ITEMS, D = embedding.shape
    H = cand_bias.shape[0]
    GROUPS = B // P
    assert GROUPS == 4 and H == P and 2 * D == P
    STEPS = 2 * T + 4 * QUAD_STEPS
    MASK_BLOCKS = -(-STEPS // P)
    REC = T + 2
    MAX_TURN = T // QUAD_STEPS + 1
    MAX_QUADS = MAX_TURN + T // QUAD_STEPS
    LATE_BLOCK = -(-MAX_TURN * QUAD_STEPS // P)
    assert 1 < LATE_BLOCK < MASK_BLOCKS
    TURN_BITS = MAX_TURN.bit_length()
    QUAD_SHIFT = QUAD_STEPS.bit_length() - 1
    COPY_BITS = 4
    EARLY = 4 * HALF_STEPS
    assert EARLY <= 2 * QUAD_STEPS
    TURN_BLOCKS = -(-(MAX_QUADS + 2) // P)

    sorted_dram = nc.dram_tensor("sorted_dram", [B, REC], I32, kind="Internal").ap()
    ended_dram = nc.dram_tensor("ended_dram", [MASK_BLOCKS * P, LANES * P], BF16, kind="Internal").ap()
    turn_dram = nc.dram_tensor("turn_dram", [TURN_BLOCKS * P, LANES * P], I32, kind="Internal").ap()

    ctx = ExitStack()
    with ctx:
        def sb(name, shape, dt):
            return ctx.enter_context(nc.sbuf_tensor(name, shape, dt))

        def pb(name):
            return ctx.enter_context(nc.psum_tensor(name, [P, COLS], F32))

        def sem(name):
            return ctx.enter_context(nc.semaphore(name))

        len_row_i = sb("len_row_i", [P, B], I32)
        key_row = sb("key_row", [P, B], F32)
        number_row = sb("number_row", [P, B], F32)
        records = sb("records", [P, GROUPS, REC], I32)
        wrap = sb("wrap", [P, GROUPS, T], F32)
        number_col = sb("number_col", [P, GROUPS], F32)
        key_col = sb("key_col", [P, GROUPS], F32)
        above = sb("above", [P, GROUPS, B], F32)
        rank_f = sb("rank_f", [P, GROUPS], F32)
        ranked = sb("ranked", [P, GROUPS, REC], I32)
        items = sb("items", [P, LANES, STEPS], I32)
        shifted = sb("shifted", [P, LANES, STEPS], I32)
        early_items = sb("early_items", [P, LANES, EARLY], I32)
        turns_first = sb("turns_first", [P, LANES], I32)
        turn_col = sb("turn_col", [P, LANES], I32)
        turn_col_1 = sb("turn_col_1", [P, LANES], I32)
        turn_col_f = sb("turn_col_f", [P, LANES], F32)
        turn_bits = sb("turn_bits", [P, TURN_BITS, LANES], I32)
        before_turn = sb("before_turn", [P, LANES, T], I32)
        upper = sb("upper", [P, GROUPS], F32)
        place_f = sb("place_f", [P, GROUPS], F32)
        place_i = sb("place_i", [P, GROUPS], I32)
        to_place = sb("to_place", [P, GROUPS, B], BF16)
        early_f = sb("early_f", [P, GROUPS, EARLY + 1], F32)
        early_rest = sb("early_rest", [P, GROUPS, EARLY + 1], F32)
        early_part = sb("early_part", [P, GROUPS, 3, EARLY + 1], BF16)
        early_sum = sb("early_sum", [P, GROUPS, 3, EARLY + 1], F32)
        early = sb("early", [P, GROUPS, EARLY + 1], I32)
        mirror = sb("mirror", [P, GROUPS], F32)
        ones = sb("ones", [P, P], F32)
        zeros = sb("zeros", [P, P], F32)
        ident = sb("ident", [P, P], F32)
        len_row = sb("len_row", [P, GROUPS, P], F32)
        len_up = sb("len_up", [P, GROUPS, P], I32)
        quad_row = sb("quad_row", [P, GROUPS, P], I32)
        turn_step = sb("turn_step", [P, LANES, P], F32)
        column_quads = sb("column_quads", [P, LANES, P], F32)
        most = sb("most", [P, 1], F32)
        counts = sb("counts", [P, 1 + LANES], I32)
        least = sb("least", [P, LANES], F32)
        second_end = sb("second_end", [P, LANES, P], F32)
        step_col = sb("step_col", [P, MASK_BLOCKS], F32)
        first_over = sb("first_over", [P, LATE_BLOCK, LANES * P], F32)
        second_on = sb("second_on", [P, LATE_BLOCK, LANES * P], F32)
        ended = sb("ended", [P, MASK_BLOCKS, LANES * P], BF16)
        turns = sb("turns", [P, TURN_BLOCKS, LANES * P], I32)
        w_x = sb("w_x", [P, 3 * H], F32)
        w_x_hi = sb("w_x_hi", [P, 3 * H], F32R)
        w_x_lo = sb("w_x_lo", [P, 3 * H], F32R)
        w_h = sb("w_h", [P, 3 * H], F32)
        bias_row = sb("bias_row", [1, 3 * H], F32)
        bias_rest = sb("bias_rest", [1, 2, 3 * H], F32)
        bias_part = sb("bias_part", [1, 4, 3 * H], BF16)
        bias_w = sb("bias_w", [4, 3 * H], BF16)
        turn_now = sb("turn_now", [P, LANES, P], I32)
        item_now = [sb(f"item_now{j}", [P, 4], I32) for j in range(2)]
        x_raw = [sb(f"x_raw{j}", [P, 4, D], F32) for j in range(2)]
        x_split = [sb(f"x_split{j}", [P, 4, 2, D], F32) for j in range(2)]
        x_parts = [sb(f"x_parts{j}", [P, COLS], F32R) for j in range(2)]
        bias_rows = [sb(f"bias_rows{j}", [4, COLS], BF16) for j in range(2)]
        h = [sb(f"h{l}", [P, P], F32) for l in range(LANES)]
        r_gate = [sb(f"r_gate{l}", [P, P], F32) for l in range(LANES)]
        u_gate = [sb(f"u_gate{l}", [P, P], F32) for l in range(LANES)]
        rh = [sb(f"rh{l}", [P, P], F32) for l in range(LANES)]
        fresh = [sb(f"fresh{l}", [P, P], F32) for l in range(LANES)]
        kept = [sb(f"kept{l}", [P, P], F32) for l in range(LANES)]
        cand = [sb(f"cand{l}", [P, P], F32) for l in range(LANES)]
        first_final = [sb(f"first_final{l}", [P, P], F32) for l in range(LANES)]
        final_rows = sb("final_rows", [P, GROUPS, H], F32)

        RC = [[pb(f"RC{l}{j}") for j in range(2)] for l in range(LANES)]
        U = [pb(f"U{l}") for l in range(LANES)]
        xT = [pb(f"xT{j}") for j in range(2)]

        s_in_len = sem("in_len")
        s_in_his = sem("in_his")
        s_in_w = sem("in_w")
        s_in_bias = sem("in_bias")
        s_bias_w = sem("bias_w_landed")
        s_const = sem("const")
        s_pool = sem("pool_chain")
        s_dve = sem("dve_chain")
        s_w_hi = sem("w_x_hi_ready")
        s_w_lo = sem("w_x_lo_ready")
        s_ends = sem("ends_ready")
        s_cleared = sem("first_final_cleared")
        s_wrapped = sem("wrapped")
        s_bias_part = sem("bias_part_ready")
        s_bias_rest = sem("bias_rest_ready")
        s_scattered = sem("scattered")
        s_ranked = sem("ranked_landed")
        s_to_place = sem("to_place_ready")
        s_lens = sem("lens_spread")
        s_len_row = sem("len_row_ready")
        s_counts = sem("counts_ready")
        s_early_parts = sem("early_parts_ready")
        s_early = sem("early_items_ready")
        s_items = sem("items_ready")
        s_ended = sem("ended_ready")
        s_ended_out = sem("ended_stored")
        s_ones_rows = sem("ones_rows_ready")
        s_item_now = sem("item_now_ready")
        s_item_seen = sem("item_now_seen")
        s_turn_seen = sem("turn_seen")
        s_loads_over = sem("loads_over")
        s_x = [sem(f"x_landed{j}") for j in range(2)]
        s_end = [sem(f"ended_landed{j}") for j in range(2)]
        s_xT = sem("xT_ready")
        s_hi = sem("hi_ready")
        s_lo = sem("lo_ready")
        s_parts = sem("x_parts_ready")
        s_xu = sem("x_update_done")
        s_h = [sem(f"h_ready{l}") for l in range(LANES)]
        s_rpre = [sem(f"r_pre{l}") for l in range(LANES)]
        s_upre = [sem(f"u_pre{l}") for l in range(LANES)]
        s_cpre = [sem(f"c_pre{l}") for l in range(LANES)]
        s_r = [sem(f"r_gate{l}") for l in range(LANES)]
        s_u = [sem(f"u_gate{l}") for l in range(LANES)]
        s_c = [sem(f"c_ready{l}") for l in range(LANES)]
        s_rh = [sem(f"rh_ready{l}") for l in range(LANES)]
        s_kept = [sem(f"kept_ready{l}") for l in range(LANES)]
        s_fresh = [sem(f"fresh_ready{l}") for l in range(LANES)]
        s_turned = sem("turns_made")
        s_turns = sem("turns_ready")
        s_turns_out = sem("turns_stored")
        s_turn = sem("turn_landed")
        s_final = sem("final_transposed")
        s_rows = sem("first_rows_ready")
        s_rows_2 = sem("second_rows_ready")
        s_act = sem("act_table")
        s_out = sem("out_stored")

        block = ctx.enter_context(nc.Block())

        def pair(lane):
            return slice(lane * HALF_STEPS * P, (lane + 1) * HALF_STEPS * P)

        def r_col(step):
            return slice(step * P, (step + 1) * P)

        def c_col(step):
            return r_col(HALF_STEPS + step)

        def quads(eng):
            eng.wait_ge(s_counts, 1)
            return eng.value_load(counts[0:1, 0:1], min_val=1, max_val=MAX_QUADS)

        @block.sync
        def _(sp):
            lens_1 = seq_lens.rearrange("(o b) -> o b", o=1)
            sp.dma_start(len_row_i[:, :], lens_1.to_broadcast([P, B])).then_inc(s_in_len, 16)
            sp.dma_start(records[:, :, T], seq_lens.rearrange("(p g) -> p g", g=GROUPS),
                         allow_slow_non_contiguous=True).then_inc(s_in_len, 16)
            sp.dma_start(records[:, :, 0:T], item_his.rearrange("(p g) t -> p g t", g=GROUPS)).then_inc(s_in_his, 16)
            for half in range(2):
                rows = slice(half * D, half * D + D)
                sp.dma_start(w_x[rows, 0:2 * H], gate_kernel[0:D, :]).then_inc(s_in_w, 16)
                sp.dma_start(w_x[rows, 2 * H:3 * H], cand_kernel[0:D, :]).then_inc(s_in_w, 16)
            sp.dma_start(w_h[:, 0:2 * H], gate_kernel[D:D + H, :]).then_inc(s_in_w, 16)
            sp.dma_start(w_h[:, 2 * H:3 * H], cand_kernel[D:D + H, :]).then_inc(s_in_w, 16)
            sp.dma_start(bias_row[:, 0:2 * H], gate_bias.rearrange("(o b) -> o b", o=1)).then_inc(s_in_bias, 16)
            sp.dma_start(bias_row[:, 2 * H:3 * H], cand_bias.rearrange("(o b) -> o b", o=1)).then_inc(s_in_bias, 16)
            sp.wait_ge(s_scattered, 16 * GROUPS)
            sp.dma_start(ranked[:, :, :], sorted_dram.rearrange("(g p) c -> p g c", p=P)).then_inc(s_ranked, 16)
            sp.wait_ge(s_bias_part, 3)
            for row in range(4):
                sp.dma_start(bias_w[row:row + 1, :], bias_part[0:1, row, :]).then_inc(s_bias_w, 16)

            def store_ended(blk):
                sp.dma_start(ended_dram[blk * P:(blk + 1) * P, :], ended[:, blk, :]).then_inc(s_ended_out, 16)

            def store_turns(blk):
                sp.wait_ge(s_turns, blk + 1)
                sp.dma_start(turn_dram[blk * P:(blk + 1) * P, :], turns[:, blk, :]).then_inc(s_turns_out, 16)

            def load_turn(quad):
                row = turn_dram[bass.ds(quad, 1), :]
                sp.dma_start(turn_now[:, :, :].rearrange("p l b -> p (l b)"),
                             row.to_broadcast([P, LANES * P])).then_inc(s_turn, 16)

            def load_ended(j, first_step):
                rows = ended_dram[bass.ds(first_step, HALF_STEPS), :].rearrange("s (l b) -> l s b", l=LANES)
                sp.dma_start(bias_rows[j][3:4, :].rearrange("o (l s b) -> o l s b", l=LANES, b=P),
                             rows.unsqueeze(0)).then_inc(s_end[j], 16)

            sp.wait_ge(s_ended, 1)
            store_ended(0)
            store_turns(0)
            sp.wait_ge(s_ones_rows, 1)
            sp.wait_ge(s_ended_out, 16)
            load_ended(0, 0)
            load_ended(1, HALF_STEPS)
            sp.wait_ge(s_turns_out, 16)
            load_turn(0)
            for blk in range(1, TURN_BLOCKS):
                store_turns(blk)
            for blk in range(1, MASK_BLOCKS):
                sp.wait_ge(s_ended, blk + 1)
                store_ended(blk)
            n = quads(sp)
            sp.wait_ge(s_ended_out, 16 * MASK_BLOCKS)
            sp.wait_ge(s_turns_out, 16 * TURN_BLOCKS)
            with sp.Fori(0, n) as q:
                sp.wait_ge(s_turned, q + 1)
                load_turn(q + 1)
                for j in range(2):
                    sp.wait_ge(s_xu, 2 * q + j + 1)
                    load_ended(j, q * QUAD_STEPS + QUAD_STEPS + j * HALF_STEPS)
            sp.wait_ge(s_end[0], 16 * n + 16)
            sp.wait_ge(s_end[1], 16 * n + 16)
            sp.wait_ge(s_turn, 16 * n + 16)
            sp.sem_inc(s_loads_over, 1)

        @block.gpsimd
        def _(pool):
            nc.gpsimd.iota(number_row[:, :], pattern=[[1, B]], base=0, channel_multiplier=0,
                           allow_small_or_imprecise_dtypes=True).then_inc(s_const, 1)
            nc.gpsimd.iota(number_col[:, :], pattern=[[1, GROUPS]], base=0, channel_multiplier=GROUPS,
                           allow_small_or_imprecise_dtypes=True).then_inc(s_const, 1)
            nc.gpsimd.iota(records[:, :, T + 1], pattern=[[1, GROUPS]], base=0,
                           channel_multiplier=GROUPS).then_inc(s_const, 1)
            chain = [0]

            def link(ins):
                chain[0] += 1
                ins.then_inc(s_pool, 1)
                pool.wait_ge(s_pool, chain[0])

            link(nc.gpsimd.memset(ident[:, :], 0.0))
            nc.gpsimd.affine_select(out=ident[:, :], in_=ident[:, :], compare_op=ALU.not_equal, fill=1.0,
                                    base=0, pattern=[[-1, P]], channel_multiplier=1).then_inc(s_const, 1)
            nc.gpsimd.memset(zeros[:, :], 0.0)
            nc.gpsimd.memset(ones[:, :], 1.0).then_inc(s_const, 1)
            nc.gpsimd.iota(step_col[:, :], pattern=[[P, MASK_BLOCKS]], base=0, channel_multiplier=1,
                           allow_small_or_imprecise_dtypes=True).then_inc(s_const, 1)
            for j in range(2):
                last = nc.gpsimd.memset(bias_rows[j][:, :], 1.0)
            last.then_inc(s_ones_rows, 1)
            nc.gpsimd.memset(items[:, :, :].rearrange("p l s -> p (l s)"), 0)
            nc.gpsimd.memset(shifted[:, :, :].rearrange("p l s -> p (l s)"), 0).then_inc(s_const, 1)
            link(nc.gpsimd.memset(bias_part[0:1, 3, :], 0.0))
            link(nc.gpsimd.memset(bias_part[0:1, 3, H:2 * H], HOLD))
            for l in range(LANES):
                last = nc.gpsimd.memset(first_final[l][:, :], 0.0)
            last.then_inc(s_cleared, 1)
            nc.gpsimd.memset(h[0][:, :], 0.0).then_inc(s_h[0], 1)
            for l in range(LANES):
                nc.gpsimd.memset(kept[l][:, :], 0.0).then_inc(s_kept[l], 1)
            nc.gpsimd.memset(u_gate[1][:, :], 1.0)
            nc.gpsimd.memset(cand[1][:, :], 0.0).then_inc(s_c[1], 1)
            for g in range(GROUPS):
                pool.wait_ge(s_wrapped, g + 1)
                pool.indirect_dma_start(sorted_dram[:, :], bass.IndirectOffsetOnAxis(place_i[:, g:g + 1], 0),
                                        records[:, g, :], None).then_inc(s_scattered, 16)

            def gather(j, k, table, first_step):
                now = nc.gpsimd.tensor_copy(item_now[j][:, :].rearrange("p (l s) -> p l s", l=LANES),
                                            table[:, :, bass.ds(first_step, HALF_STEPS)])
                now.then_inc(s_item_now, 1)
                pool.wait_ge(s_item_now, k + 1)
                pool.sem_inc(s_item_seen, 1)
                for c in range(4):
                    pool.indirect_dma_start(x_raw[j][:, c, :], None, embedding[:, :],
                                            bass.IndirectOffsetOnAxis(item_now[j][:, c:c + 1], 0)).then_inc(s_x[j], 16)

            for i, before in enumerate((bias_row[:, :], bias_rest[:, 0, :])):
                pool.wait_ge(s_bias_part, i + 1)
                link(nc.gpsimd.tensor_tensor(bias_rest[:, i, :], before, bias_part[0:1, i, :], ALU.subtract))
                pool.sem_inc(s_bias_rest, 1)
            pool.wait_ge(s_early, 1)
            gather(0, 0, early_items, 0)
            gather(1, 1, early_items, HALF_STEPS)
            pool.wait_ge(s_lo, 1)
            gather(0, 2, early_items, 2 * HALF_STEPS)
            pool.wait_ge(s_lo, 2)
            gather(1, 3, early_items, 3 * HALF_STEPS)
            n = quads(pool)
            pool.wait_ge(s_items, 1)
            with pool.Fori(0, n) as q:
                for j in range(2):
                    pool.wait_ge(s_lo, 2 * q + j + 3)
                    gather(j, 2 * q + j + 4, items, q * QUAD_STEPS + (j + 4) * HALF_STEPS)
            pool.wait_ge(s_x[1], 64 * n + 128)
            pool.sem_inc(s_loads_over, 1)

            for g in range(GROUPS):
                if g < LANES:
                    pool.wait_ge(s_rows, g + 1)
                else:
                    pool.wait_ge(s_rows_2, g + 1 - LANES)
                pool.indirect_dma_start(out[:, :], bass.IndirectOffsetOnAxis(ranked[:, g, T + 1:T + 2], 0),
                                        final_rows[:, g, :], None).then_inc(s_out, 16)
            pool.wait_ge(s_out, 16 * GROUPS)

        @block.tensor
        def _(pe):
            pe.wait_ge(s_early_parts, 1)
            for g in range(GROUPS):
                pe.wait_ge(s_to_place, g + 1)
                last = nc.tensor.matmul(xT[1][:, :], early_part[:, g, 0, EARLY:EARLY + 1].to_broadcast([P, P]),
                                        to_place[:, g, :],
                                        start=g == 0, stop=g == GROUPS - 1)
            last.then_inc(s_lens, 1)
            for to in range(GROUPS):
                cols = slice(to * 3 * (EARLY + 1), (to + 1) * 3 * (EARLY + 1))
                for g in range(GROUPS):
                    last = nc.tensor.matmul(xT[0][:, cols], to_place[:, g, to * P:(to + 1) * P], early_part[:, g, :, :].rearrange("p t c -> p (t c)"),
                                            start=to + g == 0, stop=True, skip_group_check=True)
            last.then_inc(s_lens, 1)
            pe.wait_ge(s_bias_w, 64)
            pe.wait_ge(s_w_lo, 1)
            n = quads(pe)

            def transposes(j, lane):
                for c in range(lane * HALF_STEPS, (lane + 1) * HALF_STEPS):
                    rows = x_split[j][:, c, :, :].rearrange("b t d -> b (t d)")
                    last = nc.tensor.transpose(xT[j][:, c * P:(c + 1) * P], rows, ident[:, :])
                return last

            def x_side(out_cols, gate, lane, j, start):
                w = slice(gate * H, (gate + 1) * H)
                nc.tensor.matmul(out_cols, w_x_hi[:, w], x_parts[j][:, pair(lane)], start=start, stop=False,
                                 skip_group_check=True)
                nc.tensor.matmul(out_cols, w_x_lo[:, w], x_parts[j][:, pair(lane)], start=False, stop=False,
                                 skip_group_check=True)
                return nc.tensor.matmul(out_cols, bias_w[:, w], bias_rows[j][:, pair(lane)], start=False, stop=False,
                                        skip_group_check=True)

            def x_reset(j, lane):
                return x_side(RC[lane][j][:, 0:HALF_STEPS * P], 0, lane, j, True)

            def x_candidate(j, lane):
                return x_side(RC[lane][j][:, HALF_STEPS * P:], 2, lane, j, False)

            def x_update(j, lane):
                return x_side(U[lane][:, 0:HALF_STEPS * P], 1, lane, j, True)

            def x_wait(j, k, ended_landed):
                pe.wait_ge(s_parts, LANES * k + LANES)
                pe.wait_ge(s_end[j], ended_landed)

            def recur(out_cols, gate, operand):
                w = slice(gate * H, (gate + 1) * H)
                return nc.tensor.matmul(out_cols, w_h[:, w], operand, start=False, stop=True, skip_group_check=True)

            def reset(j, step, lane, s):
                pe.wait_ge(s_h[lane], s + 1)
                recur(RC[lane][j][:, r_col(step)], 0, h[lane][:, :]).then_inc(s_rpre[lane], 1)

            def update(step, lane):
                recur(U[lane][:, r_col(step)], 1, h[lane][:, :]).then_inc(s_upre[lane], 1)

            def candidate(j, step, lane, s):
                pe.wait_ge(s_rh[lane], s + 1)
                recur(RC[lane][j][:, c_col(step)], 2, rh[lane][:, :]).then_inc(s_cpre[lane], 1)

            for k in range(2):
                pe.wait_ge(s_lo, k + 1)
                transposes(k, 0)
                transposes(k, 1).then_inc(s_xT, 1)
            x_wait(0, 0, 16)
            for l in range(LANES):
                x_reset(0, l)
            x_candidate(0, 0)
            x_update(0, 0)
            reset(0, 0, 0, 0)

            with pe.Fori(0, n) as q:
                for j in range(2):
                    i = 1 - j
                    k = 2 * q + j
                    s = q * QUAD_STEPS + j * HALF_STEPS
                    update(0, 0)
                    x_candidate(j, 1)
                    candidate(j, 0, 0, s)
                    pe.wait_ge(s_kept[1], s + 1)
                    x_update(j, 1).then_inc(s_xu, 1)
                    reset(j, 0, 1, s)
                    update(0, 1)
                    x_wait(i, k + 1, (q + j + 1) * 16)
                    x_reset(i, 0)
                    pe.wait_ge(s_lo, k + 3)
                    transposes(j, 0)
                    reset(j, 1, 0, s + 1)
                    candidate(j, 0, 1, s)
                    update(1, 0)
                    transposes(j, 1).then_inc(s_xT, 1)
                    x_reset(i, 1)
                    candidate(j, 1, 0, s + 1)
                    x_candidate(i, 0)
                    reset(j, 1, 1, s + 1)
                    update(1, 1)
                    pe.wait_ge(s_kept[0], s + 3)
                    x_update(i, 0)
                    reset(i, 0, 0, s + 2)
                    candidate(j, 1, 1, s + 1)

            pe.wait_ge(s_h[0], n * QUAD_STEPS + 1)
            pe.wait_ge(s_parts, LANES * (2 * n + 2))
            for l in range(LANES):
                nc.tensor.transpose(xT[0][:, l * P:(l + 1) * P], first_final[l][:, :], ident[:, :]).then_inc(s_final, 1)
            for l in range(LANES):
                pe.wait_ge(s_h[l], n * QUAD_STEPS + 1)
                nc.tensor.transpose(xT[1][:, l * P:(l + 1) * P], h[l][:, :], ident[:, :]).then_inc(s_final, 1)

        @block.scalar
        def _(act):
            def high_part(j, k, landed, transposed):
                act.wait_ge(s_x[j], landed)
                act.wait_ge(s_xT, transposed)
                nc.scalar.copy(x_split[j][:, :, 0, :].bitcast(F32R), x_raw[j][:, :, :]).then_inc(s_hi, 1)

            def operand(j, lane, k):
                act.wait_ge(s_xT, k + 1)
                nc.scalar.copy(x_parts[j][:, pair(lane)], xT[j][:, pair(lane)]).then_inc(s_parts, 1)

            def reset(j, step, lane, s):
                act.wait_ge(s_rpre[lane], s + 1)
                nc.scalar.activation(r_gate[lane][:, :], RC[lane][j][:, r_col(step)], ACT.Sigmoid).then_inc(s_r[lane], 1)

            def update(step, lane, s):
                act.wait_ge(s_upre[lane], s + 1)
                nc.scalar.activation(u_gate[lane][:, :], U[lane][:, r_col(step)], ACT.Sigmoid).then_inc(s_u[lane], 1)

            def candidate(j, step, lane, s):
                act.wait_ge(s_cpre[lane], s + 1)
                nc.scalar.activation(cand[lane][:, :], RC[lane][j][:, c_col(step)], ACT.Tanh).then_inc(s_c[lane], 1)

            act.wait_ge(s_const, 5)
            nc.scalar.activation(r_gate[0][:, 0:1], ones[:, 0:1], ACT.Sigmoid).then_inc(s_act, 1)
            act.wait_ge(s_in_w, 96)
            nc.scalar.copy(w_x_hi[:, :], w_x[:, :]).then_inc(s_w_hi, 1)
            act.wait_ge(s_in_bias, 32)
            for i, rest in enumerate((bias_row[:, :], bias_rest[:, 0, :], bias_rest[:, 1, :])):
                if i:
                    act.wait_ge(s_bias_rest, i)
                nc.scalar.copy(bias_part[0:1, i, :], rest).then_inc(s_bias_part, 1)
            act.wait_ge(s_lens, 1)
            nc.scalar.copy(len_row[:, :, :], xT[1][:, :].rearrange("p (g b) -> p g b", g=GROUPS)).then_inc(s_len_row, 1)
            n = quads(act)
            high_part(0, 0, 64, 0)
            high_part(1, 1, 64, 0)
            for k in range(2):
                for lane in range(LANES):
                    operand(k, lane, k)
            high_part(0, 2, 128, 1)
            reset(0, 0, 0, 0)
            with act.Fori(0, n) as q:
                for j in range(2):
                    i = 1 - j
                    k = 2 * q + j
                    s = q * QUAD_STEPS + j * HALF_STEPS
                    update(0, 0, s)
                    candidate(j, 0, 0, s)
                    high_part(i, k + 3, (q + j + 2) * 64, k + 2)
                    reset(j, 0, 1, s)
                    update(0, 1, s)
                    reset(j, 1, 0, s + 1)
                    candidate(j, 0, 1, s)
                    update(1, 0, s + 1)
                    operand(j, 0, k + 2)
                    candidate(j, 1, 0, s + 1)
                    operand(j, 1, k + 2)
                    reset(j, 1, 1, s + 1)
                    update(1, 1, s + 1)
                    reset(i, 0, 0, s + 2)
                    candidate(j, 1, 1, s + 1)
            act.wait_ge(s_final, LANES)
            for l in range(LANES):
                nc.scalar.copy(final_rows[:, l, :], xT[0][:, l * P:(l + 1) * P]).then_inc(s_rows, 1)

        @block.vector
        def _(dve):
            chain = [0]

            def link(ins):
                chain[0] += 1
                ins.then_inc(s_dve, 1)
                dve.wait_ge(s_dve, chain[0])

            dve.wait_ge(s_in_len, 32)
            dve.wait_ge(s_const, 3)
            top = float(T)
            for g_len, g_num, key in ((len_row_i[:, :], number_row[:, :], key_row[:, :]),
                                      (records[:, :, T], number_col[:, :], key_col[:, :])):
                link(nc.vector.tensor_scalar(key, g_len, top, 0.0, ALU.min, ALU.max))
                if g_len.shape[1] == GROUPS:
                    link(nc.vector.tensor_copy(early_f[:, :, EARLY], key))
                link(nc.vector.scalar_tensor_tensor(key, key, float(B), g_num, ALU.mult, ALU.subtract))
            for g in range(GROUPS):
                last = nc.vector.tensor_scalar(above[:, g, :], key_row[:, :], key_col[:, g:g + 1], None, ALU.is_gt,
                                               ALU.add, accum_out=rank_f[:, g:g + 1])
            link(last)
            link(nc.vector.tensor_scalar(upper[:, :], rank_f[:, :], float(B // 2), None, ALU.is_ge))
            link(nc.vector.tensor_scalar(mirror[:, :], rank_f[:, :], -2.0, float(B + B // 2 - 1), ALU.mult, ALU.add))
            link(nc.vector.tensor_tensor(mirror[:, :], mirror[:, :], upper[:, :], ALU.mult))
            nc.vector.tensor_tensor(place_i[:, :], rank_f[:, :], mirror[:, :], ALU.add)
            nc.vector.tensor_tensor(place_f[:, :], rank_f[:, :], mirror[:, :], ALU.add)
            dve.wait_ge(s_in_his, 16)
            for g in range(GROUPS):
                his = records[:, g, 0:T]
                link(nc.vector.tensor_scalar(wrap[:, g, :], his, 0.0, float(N_ITEMS), ALU.is_lt, ALU.mult))
                link(nc.vector.tensor_tensor(wrap[:, g, :], wrap[:, g, :], his, ALU.add))
                nc.vector.tensor_scalar(his, wrap[:, g, :], 0.0, float(N_ITEMS - 1), ALU.max,
                                        ALU.min).then_inc(s_wrapped, 1)
            dve.wait_ge(s_wrapped, GROUPS)
            dve.wait_ge(s_const, 6)
            link(nc.vector.tensor_copy(early_f[:, :, 0:EARLY], records[:, :, 0:EARLY]))
            link(nc.vector.tensor_copy(early_part[:, :, 0, :], early_f[:, :, :]))
            link(nc.vector.tensor_tensor(early_rest[:, :, :], early_f[:, :, :], early_part[:, :, 0, :], ALU.subtract))
            link(nc.vector.tensor_copy(early_part[:, :, 1, :], early_rest[:, :, :]))
            nc.vector.tensor_tensor(early_part[:, :, 2, :], early_rest[:, :, :], early_part[:, :, 1, :],
                                    ALU.subtract).then_inc(s_early_parts, 1)
            for g in range(GROUPS):
                nc.vector.tensor_scalar(to_place[:, g, :], number_row[:, :], place_f[:, g:g + 1], None,
                                        ALU.is_equal).then_inc(s_to_place, 1)
            dve.wait_ge(s_w_hi, 1)
            nc.vector.tensor_tensor(w_x_lo[:, :], w_x[:, :], w_x_hi[:, :].bitcast(F32),
                                    ALU.subtract).then_inc(s_w_lo, 1)
            first, second = slice(0, LANES), slice(LANES, 2 * LANES)
            dve.wait_ge(s_lens, 2)
            link(nc.vector.tensor_copy(early_sum[:, :, :, :], xT[0][:, 0:GROUPS * 3 * (EARLY + 1)].rearrange(
                "p (g t c) -> p g t c", g=GROUPS, t=3)))
            link(nc.vector.tensor_tensor(early_rest[:, :, :], early_sum[:, :, 1, :], early_sum[:, :, 2, :], ALU.add))
            link(nc.vector.tensor_tensor(early[:, :, :], early_rest[:, :, :], early_sum[:, :, 0, :], ALU.add))
            nc.vector.tensor_copy(early_items[:, :, :], early[:, first, 0:EARLY])
            link(nc.vector.tensor_scalar(turn_col_1[:, :], early[:, first, EARLY], QUAD_SHIFT, None,
                                         ALU.logical_shift_right))
            nc.vector.tensor_scalar(turn_col[:, :], turn_col_1[:, :], 1.0, None, ALU.add)
            link(nc.vector.tensor_scalar(turns_first[:, :], turn_col_1[:, :], 0.0, None, ALU.is_equal))
            nc.vector.copy_predicated(early_items[:, :, QUAD_STEPS:],
                                      turns_first[:, :].unsqueeze(2).to_broadcast([P, LANES, EARLY - QUAD_STEPS]),
                                      early[:, second, 0:EARLY - QUAD_STEPS]).then_inc(s_early, 1)
            for k in range(TURN_BITS):
                nc.vector.tensor_scalar(turn_bits[:, k, :], turn_col[:, :], k, 1,
                                        ALU.logical_shift_right, ALU.bitwise_and)
            link(nc.vector.tensor_scalar(turn_col_f[:, :], turn_col[:, :], float(QUAD_STEPS), None, ALU.mult))
            for l in range(LANES):
                link(nc.vector.tensor_scalar(before_turn[:, l, :], number_row[:, 0:T], turn_col_f[:, l:l + 1], None,
                                             ALU.is_lt))
            dve.wait_ge(s_len_row, 1)
            nc.vector.tensor_scalar(len_up[:, first, :], len_row[:, first, :], float(QUAD_STEPS), None, ALU.add)
            link(nc.vector.tensor_scalar(len_up[:, second, :], len_row[:, second, :], float(QUAD_STEPS - 1), None,
                                         ALU.add))
            link(nc.vector.tensor_scalar(quad_row[:, :, :], len_up[:, :, :], QUAD_SHIFT, None, ALU.logical_shift_right))
            turn_row = quad_row[:, first, :]
            nc.vector.tensor_scalar(turn_step[:, :, :], turn_row, float(QUAD_STEPS), None, ALU.mult)
            link(nc.vector.tensor_tensor(column_quads[:, :, :], turn_row, quad_row[:, second, :], ALU.add))
            nc.vector.reduce_max(most[:, :], column_quads[:, :, :], AX.XY)
            link(nc.vector.tensor_reduce(least[:, :], turn_row, AX.X, ALU.min))
            nc.vector.tensor_scalar(counts[:, 1:1 + LANES], least[:, :], -1.0, None, ALU.add)
            nc.vector.tensor_copy(counts[:, 0:1], most[:, :]).then_inc(s_counts, 1)
            nc.vector.tensor_tensor(second_end[:, :, :], len_row[:, second, :], turn_step[:, :, :],
                                    ALU.add).then_inc(s_ends, 1)
            dve.wait_ge(s_ends, 1)

            def flat(row):
                return row.rearrange("p l b -> p (l b)")

            def ended_blocks(begin, end):
                now = [step_col[:, blk:blk + 1] for blk in range(MASK_BLOCKS)]
                for blk in range(begin, end):
                    last = nc.vector.tensor_scalar(first_over[:, blk, :], flat(len_row[:, first, :]), now[blk], None,
                                                   ALU.is_le)
                link(last)
                for blk in range(begin, end):
                    last = nc.vector.scalar_tensor_tensor(second_on[:, blk, :], flat(turn_step[:, :, :]), now[blk],
                                                          first_over[:, blk, :], ALU.is_le, ALU.subtract)
                link(last)
                for blk in range(begin, end):
                    nc.vector.scalar_tensor_tensor(ended[:, blk, :], flat(second_end[:, :, :]), now[blk],
                                                   second_on[:, blk, :], ALU.is_le, ALU.subtract).then_inc(s_ended, 1)

            def late_ended_block(blk):
                nc.vector.tensor_scalar(ended[:, blk, :], flat(second_end[:, :, :]), step_col[:, blk:blk + 1], None,
                                        ALU.is_le).then_inc(s_ended, 1)

            def turns_block(blk):
                nc.vector.tensor_scalar(turns[:, blk, :].rearrange("p (l b) -> p l b", l=LANES), turn_row,
                                        step_col[:, blk:blk + 1], None, ALU.is_equal).then_inc(s_turns, 1)

            def low_part(j, k):
                dve.wait_ge(s_hi, k + 1)
                nc.vector.tensor_tensor(x_split[j][:, :, 1, :], x_raw[j][:, :, :], x_split[j][:, :, 0, :],
                                        ALU.subtract).then_inc(s_lo, 1)

            ended_blocks(0, 1)
            for blk in range(TURN_BLOCKS):
                turns_block(blk)
            ended_blocks(1, LATE_BLOCK)
            low_part(0, 0)
            for blk in range(LATE_BLOCK, MASK_BLOCKS):
                late_ended_block(blk)
            n = quads(dve)
            lane_0_begins, lane_1_begins = (
                dve.value_load(counts[0:1, 1 + l:2 + l], min_val=0, max_val=MAX_TURN - 1) for l in range(LANES))
            dve.wait_ge(s_ranked, 16)
            dve.wait_ge(s_const, 7)
            src, reach = ranked[:, second, 0:T], T
            for k in range(TURN_BITS):
                shift = QUAD_STEPS << k
                bit = turn_bits[:, k, :].unsqueeze(2)
                if k < COPY_BITS:
                    dst = items if k % 2 == (COPY_BITS - 1) % 2 else shifted
                    link(nc.vector.tensor_copy(dst[:, :, 0:reach], src[:, :, 0:reach]))
                    link(nc.vector.copy_predicated(dst[:, :, shift:shift + reach], bit.to_broadcast([P, LANES, reach]),
                                                   src[:, :, 0:reach]))
                    src = dst
                else:
                    to = min(STEPS, reach + shift)
                    while to > shift:
                        begin = max(shift, (to - 1) // shift * shift)
                        link(nc.vector.copy_predicated(items[:, :, begin:to], bit.to_broadcast([P, LANES, to - begin]),
                                                       items[:, :, begin - shift:to - shift]))
                        to = begin
                reach = min(STEPS, reach + shift)
                if k == 1:
                    low_part(1, 1)
                if k == TURN_BITS - 2:
                    low_part(0, 2)
            nc.vector.copy_predicated(items[:, :, 0:T], before_turn[:, :, :], ranked[:, first, 0:T]).then_inc(s_items, 1)
            dve.wait_ge(s_cleared, 1)

            def reset(lane, s):
                dve.wait_ge(s_r[lane], s + 1)
                nc.vector.tensor_tensor(rh[lane][:, :], r_gate[lane][:, :], h[lane][:, :],
                                        ALU.mult).then_inc(s_rh[lane], 1)

            def keep(lane, s):
                dve.wait_ge(s_u[lane], s + 1)
                nc.vector.tensor_tensor(kept[lane][:, :], u_gate[lane][:, :], h[lane][:, :],
                                        ALU.mult).then_inc(s_kept[lane], 1)

            def put_away(lane, s):
                dve.wait_ge(s_h[lane], s + 1)
                dve.sem_inc(s_turn_seen, 1)
                nc.vector.copy_predicated(first_final[lane][:, :], turn_now[:, lane, :], h[lane][:, :])

            def drop(lane, count):
                dve.wait_ge(s_kept[lane], count)
                dve.sem_inc(s_turn_seen, 1)
                return nc.vector.copy_predicated(kept[lane][:, :], turn_now[:, lane, :], zeros[:, :])

            def blend(lane, count):
                dve.wait_ge(s_c[lane], count)
                nc.vector.scalar_tensor_tensor(fresh[lane][:, :], u_gate[lane][:, :], 1.0, cand[lane][:, :],
                                               ALU.subtract, ALU.mult).then_inc(s_fresh[lane], 1)

            def new_state(lane, count):
                dve.wait_ge(s_fresh[lane], count)
                nc.vector.tensor_tensor(h[lane][:, :], kept[lane][:, :], fresh[lane][:, :],
                                        ALU.subtract).then_inc(s_h[lane], 1)

            def quad(q, turning, last_of_1=False):
                for j in range(2):
                    for step in range(HALF_STEPS):
                        s = q * QUAD_STEPS + j * HALF_STEPS + step
                        begins = j == 0 and step == 0
                        ends = j == 1 and step == HALF_STEPS - 1
                        reset(0, s)
                        if ends:
                            dve.wait_ge(s_turn, 16 * q + 32)
                            dve.sem_inc(s_turn_seen, 1)
                        if begins and 1 in turning:
                            dve.wait_ge(s_turn, 16 * q + 16)
                            drop(1, s + 1).then_inc(s_turned, 1)
                        blend(1, s + 1)
                        if ends and 0 in turning:
                            keep(0, s)
                            new_state(1, s + 1)
                            drop(0, s + 2)
                            put_away(0, s)
                        else:
                            new_state(1, s + 1)
                            keep(0, s)
                        if ends and 1 in turning:
                            put_away(1, s)
                        blend(0, s + 1)
                        new_state(0, s + 1)
                        if begins and 1 not in turning:
                            dve.wait_ge(s_turn, 16 * q + 16)
                            dve.wait_ge(s_fresh[1], s + 1)
                            dve.sem_inc(s_turned, 1)
                        reset(1, s)
                        keep(1, s)
                        if ends and last_of_1:
                            drop(1, s + 2)
                        if j != step:
                            low_part(1 - j, 2 * q + j + 3)

            with dve.If(lane_1_begins > 0):
                with dve.Fori(0, lane_1_begins) as q:
                    quad(q, ())
            with dve.If(lane_0_begins > lane_1_begins):
                with dve.Fori(lane_1_begins, lane_0_begins) as q:
                    quad(q, (1,))
            quad(lane_0_begins, (0, 1), last_of_1=True)
            with dve.If(n > lane_0_begins + 1):
                with dve.Fori(lane_0_begins + 1, n) as q:
                    quad(q, (0,))
            blend(1, n * QUAD_STEPS + 1)
            new_state(1, n * QUAD_STEPS + 1)
            dve.wait_ge(s_final, GROUPS)
            for l in range(LANES):
                nc.vector.tensor_copy(final_rows[:, LANES + l, :], xT[1][:, l * P:(l + 1) * P]).then_inc(s_rows_2, 1)


_INS = ["r_item_his", "r_seq_lens", "L0_rec_embedding", "L0_rec_gate_kernel", "L0_rec_gate_bias",
        "L0_rec_cand_kernel", "L0_rec_cand_bias"]


def kernel(**inputs):
    import numpy as _np
    import concourse.bacc as _bacc
    from concourse import mybir as _mybir
    from concourse.bass_utils import run_bass_kernel_spmd as _run

    nc = _bacc.Bacc("TRN2", target_bir_lowering=False, num_devices=1)
    arrays, args = {}, []
    for name in _INS:
        a = _np.ascontiguousarray(inputs[name])
        arrays[f"in_{name}_dram"] = a
        args.append(nc.dram_tensor(f"in_{name}_dram", a.shape, _mybir.dt.from_np(a.dtype), kind="ExternalInput").ap())
    shape = (inputs["r_item_his"].shape[0], inputs["L0_rec_cand_bias"].shape[0])
    args.append(nc.dram_tensor("out_0_dram", shape, _mybir.dt.float32, kind="ExternalOutput").ap())
    gru_kernel(nc, *args)
    r = _run(nc, [arrays], core_ids=[0])
    return r.results[0]["out_0_dram"]
```
